# Optimizing a Trainium2 kernel written in Bass

```python
import numpy as np
import jax
import jax.numpy as jnp

def _softmax(x, axis=-1):
    return jax.nn.softmax(x, axis=axis)

def _gelu(x):
    return jax.nn.gelu(x, approximate=True)

def _silu(x):
    return jax.nn.silu(x)

def _sigmoid(x):
    return jax.nn.sigmoid(x)

def _layernorm(x, axis=-1, eps=1e-05):
    m = jnp.mean(x, axis=axis, keepdims=True)
    v = jnp.var(x, axis=axis, keepdims=True)
    return (x - m) / jnp.sqrt(v + eps)

def _scatter_add(tgt, idx, src, axis=0):
    return tgt.at[idx].add(src)

def _segment_sum(src, seg, n):
    return jax.ops.segment_sum(src, seg, n)
kernel_name = 'mk_seq_postln_d1_jaxref_r4_fe2dde'

def setup_inputs(seed: int=0):
    np.random.seed(seed)
    _w = jnp.asarray

    def _L0_attn_setup():
        import jax, jax.numpy as jnp
        import numpy as np
        import math
        NUM_HEADS = 16
        ATTN_WIDTH = 64
        key = jax.random.key(seed)
        ks = jax.random.split(key, 5)
        B, S, C, H = (2, 512, 256, 256)
        scale = 0.02
        return {'x': jax.random.normal(ks[0], (B, S, C), dtype=jnp.float32), 'Wq': jax.random.normal(ks[1], (C, H), dtype=jnp.float32) * scale, 'Wk': jax.random.normal(ks[2], (C, H), dtype=jnp.float32) * scale, 'Wv': jax.random.normal(ks[3], (C, H), dtype=jnp.float32) * scale, 'Wo': jax.random.normal(ks[4], (H, C), dtype=jnp.float32) * scale}
    _L0_attn_in = _L0_attn_setup()

    def _L0_ffn_setup():
        import jax, jax.numpy as jnp
        import numpy as np
        LATENT = 256
        LEAF_W = 64
        DEPTH = 4
        N_LEAVES = 2 ** DEPTH
        N_NODES = 2 ** DEPTH - 1
        B, S = (4, 512)

        def _fff_params(key, prefix):
            ks = jax.random.split(key, 4)
            d, h, l, n = (LATENT, LEAF_W, N_LEAVES, N_NODES)
            s_in = 1.0 / np.sqrt(d).astype(np.float32)
            s_h = 1.0 / np.sqrt(h).astype(np.float32)
            return {f'{prefix}_node_w': jax.random.normal(ks[0], (n, d), jnp.float32) * s_in, f'{prefix}_node_b': jax.random.normal(ks[1], (n,), jnp.float32) * s_in, f'{prefix}_w1': jax.random.normal(ks[2], (l, d, h), jnp.float32) * s_in, f'{prefix}_b1': jnp.zeros((l, h), jnp.float32), f'{prefix}_w2': jax.random.normal(ks[3], (l, h, d), jnp.float32) * s_h, f'{prefix}_b2': jnp.zeros((l, d), jnp.float32)}

        def _fff(x, node_w, node_b, w1, b1, w2, b2):
            Bx, Sx, D = x.shape
            xf = x.reshape(-1, D)
            N = xf.shape[0]
            cur = jnp.zeros((N,), jnp.int32)
            for _ in range(DEPTH):
                pw = node_w[cur]
                score = jnp.einsum('nd,nd->n', xf, pw) + node_b[cur]
                cur = 2 * cur + 1 + (score >= 0).astype(jnp.int32)
            leaf = cur - N_NODES
            sel = jax.nn.one_hot(leaf, N_LEAVES, dtype=xf.dtype)
            hidden_all = jax.nn.relu(jnp.einsum('nd,ldh->lnh', xf, w1) + b1[:, None, :])
            hidden = hidden_all * sel.T[:, :, None]
            out = jnp.einsum('lnh,lho->no', hidden, w2) + sel @ b2
            return out.reshape(Bx, Sx, D)
        key = jax.random.key(seed)
        kx, kq, kk, kv = jax.random.split(key, 4)
        inp = {'x': jax.random.normal(kx, (B, S, LATENT), jnp.float32)}
        inp.update(_fff_params(kq, 'q'))
        inp.update(_fff_params(kk, 'k'))
        inp.update(_fff_params(kv, 'v'))
        return inp
    _L0_ffn_in = _L0_ffn_setup()
    _d = {'L0_attn_x': _L0_attn_in['x'], 'L0_attn_Wq': _L0_attn_in['Wq'], 'L0_attn_Wk': _L0_attn_in['Wk'], 'L0_attn_Wv': _L0_attn_in['Wv'], 'L0_attn_Wo': _L0_attn_in['Wo'], 'L0_ffn_q_node_w': _L0_ffn_in['q_node_w'], 'L0_ffn_q_node_b': _L0_ffn_in['q_node_b'], 'L0_ffn_q_w1': _L0_ffn_in['q_w1'], 'L0_ffn_q_b1': _L0_ffn_in['q_b1'], 'L0_ffn_q_w2': _L0_ffn_in['q_w2'], 'L0_ffn_q_b2': _L0_ffn_in['q_b2'], 'L0_ffn_k_node_w': _L0_ffn_in['k_node_w'], 'L0_ffn_k_node_b': _L0_ffn_in['k_node_b'], 'L0_ffn_k_w1': _L0_ffn_in['k_w1'], 'L0_ffn_k_b1': _L0_ffn_in['k_b1'], 'L0_ffn_k_w2': _L0_ffn_in['k_w2'], 'L0_ffn_k_b2': _L0_ffn_in['k_b2'], 'L0_ffn_v_node_w': _L0_ffn_in['v_node_w'], 'L0_ffn_v_node_b': _L0_ffn_in['v_node_b'], 'L0_ffn_v_w1': _L0_ffn_in['v_w1'], 'L0_ffn_v_b1': _L0_ffn_in['v_b1'], 'L0_ffn_v_w2': _L0_ffn_in['v_w2'], 'L0_ffn_v_b2': _L0_ffn_in['v_b2']}
    _x0 = _d['L0_attn_x']
    _d['L0_attn_x'] = jax.random.normal(jax.random.fold_in(jax.random.key(seed), 1), (8, 1024, 256), dtype=_x0.dtype)
    del _x0
    return _d

def reference(L0_attn_x, L0_attn_Wq, L0_attn_Wk, L0_attn_Wv, L0_attn_Wo, L0_ffn_q_node_w, L0_ffn_q_node_b, L0_ffn_q_w1, L0_ffn_q_b1, L0_ffn_q_w2, L0_ffn_q_b2, L0_ffn_k_node_w, L0_ffn_k_node_b, L0_ffn_k_w1, L0_ffn_k_b1, L0_ffn_k_w2, L0_ffn_k_b2, L0_ffn_v_node_w, L0_ffn_v_node_b, L0_ffn_v_w1, L0_ffn_v_b1, L0_ffn_v_w2, L0_ffn_v_b2):

    def _L0_attn_ref(x, Wq, Wk, Wv, Wo):
        import jax, jax.numpy as jnp
        import numpy as np
        import math
        NUM_HEADS = 16
        ATTN_WIDTH = 64
        B, S, C = x.shape
        H = NUM_HEADS
        dh = Wq.shape[1] // H

        def split_heads(t):
            return t.reshape(B, S, H, dh).transpose(0, 2, 1, 3)
        q = split_heads(x @ Wq)
        k = split_heads(x @ Wk)
        v = split_heads(x @ Wv)
        scores = jnp.einsum('bhqd,bhkd->bhqk', q, k) / math.sqrt(dh)
        scores = jnp.exp(scores - jnp.max(scores, axis=-1, keepdims=True))
        i = jnp.arange(S)[:, None]
        j = jnp.arange(S)[None, :]
        d = j - i
        half = ATTN_WIDTH // 2
        mask = (d <= half - 1) & (d >= -half)
        scores = jnp.where(mask, scores, 0.0)
        weights = jax.nn.softmax(scores, axis=-1)
        out = jnp.einsum('bhqk,bhkd->bhqd', weights, v)
        out = out.transpose(0, 2, 1, 3).reshape(B, S, H * dh)
        return out @ Wo

    def _L0_ffn_ref(x, q_node_w, q_node_b, q_w1, q_b1, q_w2, q_b2, k_node_w, k_node_b, k_w1, k_b1, k_w2, k_b2, v_node_w, v_node_b, v_w1, v_b1, v_w2, v_b2):
        import jax, jax.numpy as jnp
        import numpy as np
        LATENT = 256
        LEAF_W = 64
        DEPTH = 4
        N_LEAVES = 2 ** DEPTH
        N_NODES = 2 ** DEPTH - 1
        B, S = (4, 512)

        def _fff_params(key, prefix):
            ks = jax.random.split(key, 4)
            d, h, l, n = (LATENT, LEAF_W, N_LEAVES, N_NODES)
            s_in = 1.0 / np.sqrt(d).astype(np.float32)
            s_h = 1.0 / np.sqrt(h).astype(np.float32)
            return {f'{prefix}_node_w': jax.random.normal(ks[0], (n, d), jnp.float32) * s_in, f'{prefix}_node_b': jax.random.normal(ks[1], (n,), jnp.float32) * s_in, f'{prefix}_w1': jax.random.normal(ks[2], (l, d, h), jnp.float32) * s_in, f'{prefix}_b1': jnp.zeros((l, h), jnp.float32), f'{prefix}_w2': jax.random.normal(ks[3], (l, h, d), jnp.float32) * s_h, f'{prefix}_b2': jnp.zeros((l, d), jnp.float32)}

        def _fff(x, node_w, node_b, w1, b1, w2, b2):
            Bx, Sx, D = x.shape
            xf = x.reshape(-1, D)
            N = xf.shape[0]
            cur = jnp.zeros((N,), jnp.int32)
            for _ in range(DEPTH):
                pw = node_w[cur]
                score = jnp.einsum('nd,nd->n', xf, pw) + node_b[cur]
                cur = 2 * cur + 1 + (score >= 0).astype(jnp.int32)
            leaf = cur - N_NODES
            sel = jax.nn.one_hot(leaf, N_LEAVES, dtype=xf.dtype)
            hidden_all = jax.nn.relu(jnp.einsum('nd,ldh->lnh', xf, w1) + b1[:, None, :])
            hidden = hidden_all * sel.T[:, :, None]
            out = jnp.einsum('lnh,lho->no', hidden, w2) + sel @ b2
            return out.reshape(Bx, Sx, D)
        q = _fff(x, q_node_w, q_node_b, q_w1, q_b1, q_w2, q_b2)
        k = _fff(x, k_node_w, k_node_b, k_w1, k_b1, k_w2, k_b2)
        v = _fff(x, v_node_w, v_node_b, v_w1, v_b1, v_w2, v_b2)
        scale = 1.0 / np.sqrt(LATENT).astype(np.float32)
        attn = jax.nn.softmax(jnp.einsum('bqd,bkd->bqk', q, k) * scale, axis=-1)
        return jnp.einsum('bqk,bkd->bqd', attn, v)
    x = L0_attn_x
    x = _layernorm(x + _L0_attn_ref(x, L0_attn_Wq, L0_attn_Wk, L0_attn_Wv, L0_attn_Wo), axis=-1)
    x = _layernorm(x + _L0_ffn_ref(x, L0_ffn_q_node_w, L0_ffn_q_node_b, L0_ffn_q_w1, L0_ffn_q_b1, L0_ffn_q_w2, L0_ffn_q_b2, L0_ffn_k_node_w, L0_ffn_k_node_b, L0_ffn_k_w1, L0_ffn_k_b1, L0_ffn_k_w2, L0_ffn_k_b2, L0_ffn_v_node_w, L0_ffn_v_node_b, L0_ffn_v_w1, L0_ffn_v_b1, L0_ffn_v_w2, L0_ffn_v_b2), axis=-1)
    return x

_drawn_inputs = setup_inputs


def setup_inputs(seed=0):
    import zlib

    import numpy as np

    out = dict(_drawn_inputs(seed))
    spreads = {'L0_ffn_q_b1': (0.0, 0.8),
     'L0_ffn_q_b2': (0.0, 0.8),
     'L0_ffn_k_b1': (0.0, 0.8),
     'L0_ffn_k_b2': (0.0, 0.8),
     'L0_ffn_v_b1': (0.0, 0.628),
     'L0_ffn_v_b2': (0.0, 0.324)}
    factors = {'L0_attn_Wq': 8.0,
     'L0_attn_Wk': 8.0,
     'L0_attn_Wv': 8.0,
     'L0_attn_Wo': 8.0,
     'L0_ffn_q_node_w': 4.778,
     'L0_ffn_q_node_b': 8.0,
     'L0_ffn_q_w1': 5.577,
     'L0_ffn_q_w2': 4.635,
     'L0_ffn_k_node_w': 4.694,
     'L0_ffn_k_node_b': 8.0,
     'L0_ffn_k_w1': 5.46,
     'L0_ffn_k_w2': 4.635,
     'L0_ffn_v_node_b': 4.153}
    for name, (base, spread) in spreads.items():
        noise = np.random.default_rng([zlib.crc32(name.encode()), seed]).standard_normal(out[name].shape)
        drawn = base * np.exp(spread * noise) if base else spread * noise
        out[name] = jnp.asarray(drawn.astype(out[name].dtype))
    for name, factor in factors.items():
        out[name] = (out[name] * factor).astype(out[name].dtype)
    return out
```

```python
from contextlib import ExitStack

import concourse.bass as bass
from concourse import mybir
from concourse.alu_op_type import AluOpType as ALU

ACT = mybir.ActivationFunctionType
F32 = mybir.dt.float32
F32R = mybir.dt.float32r
BF16 = mybir.dt.bfloat16

P = 128
LN_EPS = 1e-5

B, S, C = 8, 1024, 256
HEADS, DH = 16, 16
WIN = 64
HALO = WIN // 2
QT = S // P
NBLK = S // WIN
GH = 8
DV = DH + 1
XPAD = HALO + S + (P - HALO)
VT = XPAD // P
KPAD = HALO + S + HALO
STEPS = GH * QT
SPLIT_ROWS = 6 * DH
ROWS = SPLIT_ROWS + 3

JOBS = {
    0: ["m", "T0", "T1", "q0", "q1", "k0", "k1", "d0", "V0", "V1", "V2", "V3", "V4", "S0"],
    1: ["m", "T0", "T1", "X0", "X1", "X2", "X3", "q0", "q1", "k0", "k1", "d0", "O0", "O1", "O2", "O3"],
}
PROJ = "qkd"
STACK_INC = 16 * 9


def present(kind, b, g):
    u = 2 * b + g
    return {
        "m": 1 <= u <= 2 * B,
        "T": 2 <= u <= 2 * B + 1,
        "q": u + 1 < 2 * B, "k": u + 1 < 2 * B, "d": u + 1 < 2 * B,
        "X": b + 1 < B,
        "V": 0 <= b < B, "S": 0 <= b < B,
        "O": 1 <= b <= B,
    }[kind]


def counted(kinds, b, g, j):
    n = 0
    for bb in range(-1, B + 1):
        for gg in (0, 1):
            if bb == -1 and gg == 0:
                continue
            for jj, name in enumerate(JOBS[gg]):
                if (bb, gg, jj) >= (b, g, j):
                    return n
                if name[0] in kinds and present(name[0], bb, gg):
                    n += 1
    return n


def before(kinds, b, g, j):
    if isinstance(b, int):
        return counted(kinds, b, g, j)
    return counted(kinds, 2, g, j) + (b - 2) * (counted(kinds, 3, 0, 0) - counted(kinds, 2, 0, 0))


ALL_JOBS = "mTqkdXVSO"
SPLIT_JOBS = "mTqkdX"


def wait(eng, sem, value):
    if isinstance(value, int) and value <= 0:
        return
    eng.wait_ge(sem, value)


def alone(eng):
    eng.nop(nofuse=True)


def wait_alone(eng, sem, value):
    if not isinstance(value, int) or value > 0:
        eng.wait_ge(sem, value)
        alone(eng)


def window_attention(nc, x, w_q, w_k, w_v, w_o, x1):
    with ExitStack() as ctx:
        def sb(name, shape, dt=F32):
            return ctx.enter_context(nc.sbuf_tensor(name, shape, dt))

        def psum(name, shape):
            return ctx.enter_context(nc.psum_tensor(name, shape, F32))

        def sem(name):
            return ctx.enter_context(nc.semaphore(name))

        ident = sb("ident", [P, P])
        ones = sb("ones", [P, P])
        window = sb("window", [P, WIN])
        neg_half = sb("neg_half", [P, QT])
        w_hi = sb("w_hi", [P, 5, 2, C], F32R)
        w_lo = sb("w_lo", [P, 5, 2, C], F32R)
        x_in = sb("x_in", [P, QT, C])
        xt_hi = sb("xt_hi", [P, 2, XPAD], F32R)
        xt_lo = sb("xt_lo", [P, 2, XPAD], F32R)
        q_parts = sb("q_parts", [P, 3, S], BF16)
        k_parts = sb("k_parts", [P, 3, S], BF16)
        d_parts = sb("d_parts", [P, 3, S // 2], BF16)
        rest = sb("rest", [P, S // 2])
        q_stack = [sb(f"q_stack{g}", [P, GH, S], BF16) for g in (0, 1)]
        k_stack = [sb(f"k_stack{g}", [P, GH, KPAD], BF16) for g in (0, 1)]
        d_stack = sb("d_stack", [P, GH, S // 2], BF16)
        above = sb("above", [P, 4, S // 2])
        row_max = [sb(f"row_max{g}", [P, STEPS]) for g in (0, 1)]
        m_parts = sb("m_parts", [STEPS, 3, P], BF16)
        m_rest = sb("m_rest", [STEPS, P])
        v_tiles = sb("v_tiles", [P, VT, HEADS, DV])
        v_win = [sb(f"v_win{g}", [P, NBLK, GH, DV]) for g in (0, 1)]
        v_sum = [sb(f"v_sum{g}", [P, HEADS, DV]) for g in (0, 1)]
        w_win = sb("w_win", [P, 2, S])
        w_raw = w_win[:].rearrange("p n (a c) -> p n a c", c=C).rearrange("p n (m a) c -> p (n m) a c", a=2)
        total = sb("total", [P, 2, 2 * QT, DV])
        inv = sb("inv", [P, 2, 2 * QT])
        att = sb("att", [P, QT, P])
        at_hi = sb("at_hi", [P, 2, S], F32R)
        at_lo = sb("at_lo", [P, 2, S], F32R)
        y = x_in
        stats = sb("stats", [P, QT, 6])
        mean_var = sb("mean_var", [P, QT, 2])
        var_eps = sb("var_eps", [P, QT])
        rstd = sb("rstd", [P, QT])
        
        p_diff = [psum(f"p_diff{i}", [P, 512]) for i in (0, 1)]
        p_half = [psum(f"p_half{i}", [P, 512]) for i in (0, 1)]
        p_win = psum("p_win", [P, S])
        p_pv = psum("p_pv", [P, 512])
        p_job = psum("p_job", [P, 512])

        s_w = sem("weights_loaded")
        s_const = sem("constants_step")
        s_whi = sem("weights_hi")
        s_wlo = sem("weights_lo")
        s_x = sem("x_loaded")
        s_xres = sem("x_res_loaded")
        s_jmm = sem("job_products")
        s_jact = sem("job_hi_part")
        s_jdone = sem("job_results_out_of_the_bank")
        s_mid = sem("proj_mid")
        s_parts = sem("proj_parts")
        s_mmid = sem("max_mid")
        s_mparts = sem("max_parts")
        s_mrow = sem("max_rows_stored")
        s_stack = [sem(f"stack_loaded{h}") for h in range(GH)]
        s_diff = sem("diff_scores")
        s_half = sem("half_scores")
        s_above = sem("above_ready")
        s_max = sem("row_max_done")
        s_win = sem("window_scores")
        s_e1 = sem("first_exp")
        s_e2 = sem("second_exp")
        s_ww = sem("window_weights")
        s_pv = sem("pv_done")
        s_tot = sem("totals")
        s_inv = sem("inverse")
        s_att = sem("attention_pair")
        s_vsum1 = sem("v_sum_copied")
        s_vwin = [sem(f"v_win_loaded{g}") for g in (0, 1)]
        s_stats = sem("stats_ready")
        s_mv = sem("mean_var_ready")
        s_veps = sem("var_eps_ready")
        s_rstd = sem("rstd_ready")
        s_norm = sem("x1_ready")
        s_store = sem("x1_stored")

        block = ctx.enter_context(nc.Block())

        def x_tiles(t, b):
            return t[bass.ds(b, 1), :, :].rearrange("o (t p) c -> p (o t) c", p=P)

        def batches(eng, unit):
            unit(-1, 1)
            unit(0, 0)
            unit(0, 1)
            unit(1, 0)
            unit(1, 1)
            with eng.Fori(2, B - 1) as b:
                unit(b, 0)
                unit(b, 1)
            unit(B - 1, 0)
            unit(B - 1, 1)
            unit(B, 0)
            unit(B, 1)

        def has(b, lo, hi):
            return (lo <= b < hi) if isinstance(b, int) else lo <= 2 and hi > 6

        def flags(b, g):
            if not isinstance(b, int):
                return True, True
            return 0 <= b < B, 1 <= 2 * b + g <= 2 * B

        def job_at(step, lag):
            s = step - 1 - lag
            return s // 4 if s >= 0 and s % 4 == 0 else None

        def jobs(b, g, step, lag):
            j = job_at(step, lag)
            if j is not None and j < len(JOBS[g]):
                name = JOBS[g][j]
                bb = b if isinstance(b, int) else 2
                if present(name[0], bb, g):
                    yield j, name[0], int(name[1:] or 0)

        def late(step, lag, steps=STEPS):
            return [h for h in range(GH) if min(QT * h + lag, steps - 1) == step]

        @block.sync
        def _(sp):
            for i, w in enumerate((w_q, w_k, w_v, w_o)):
                sp.dma_start(w_raw[:, i], w.rearrange("(a p) n -> p a n", p=P)).then_inc(s_w, 16)
            wait_alone(sp, s_const, 17)

            def unit(b, g):
                cur, prev = flags(b, g)
                u = 2 * b + g
                if prev:
                    wait_alone(sp, s_mparts, u)
                    for part in range(3):
                        row = SPLIT_ROWS + part
                        sp.dma_start(q_stack[1 - g][row:row + 1, :, :],
                                     m_parts[:, part, :]).then_inc(s_mrow, 16)
                if g == 1 and has(b, -1, 0):
                    sp.dma_start(x_in[:], x_tiles(x, 0)).then_inc(s_x, 16)
                if g == 0 and has(b, 2, B + 1):
                    store(b - 2)
                    wait_alone(sp, s_store, 16 * (b - 1))
                if g == 0 and has(b, 0, B - 1):
                    wait_alone(sp, s_jmm, before(ALL_JOBS, b, 0, 0))
                    sp.dma_start(x_in[:], x_tiles(x, b + 1)).then_inc(s_x, 16)
                if g == 1 and has(b, 0, B):
                    values(b, 1)
                if g == 1 and isinstance(b, int) and b == B:
                    residual(b)
                for h in range(GH):
                    if g == 1 and h == 4 and has(b, 1, B):
                        residual(b)
                    if g == 0 and h == 6 and has(b, 0, B):
                        values(b, 0)
                    if has(b, -1, B) and not (isinstance(b, int) and u + 1 >= 2 * B):
                        load_stack(b, g, h)

            def residual(b):
                wait_alone(sp, s_jmm, before(ALL_JOBS, b, 1, JOBS[1].index("X3") + 1))
                sp.dma_start(y[:], x_tiles(x, b - 1)).then_inc(s_xres, 16)

            def values(b, g):
                wait_alone(sp, s_jdone, before(ALL_JOBS, b, 0, JOBS[0].index("V4")) + 1)
                wait_alone(sp, s_pv, GH * (2 * b + g - 1))
                hs = slice(GH * g, GH * g + GH)
                sp.dma_start(v_win[g][:, 0::2], v_tiles[:, 0:VT - 1, hs]).then_inc(s_vwin[g], 16)
                sp.dma_start(v_win[g][0:64, 1::2], v_tiles[64:P, 0:VT - 1, hs]).then_inc(s_vwin[g], 16)
                sp.dma_start(v_win[g][64:P, 1::2], v_tiles[0:64, 1:VT, hs]).then_inc(s_vwin[g], 16)

            def load_stack(b, g, h):
                u = 2 * b + g
                n = 1 - g
                if h == 0:
                    wait_alone(sp, s_parts, 5 * (u + 2))
                wait_alone(sp, s_win, GH * (u - 1) + h + 1)
                wait_alone(sp, s_diff, STEPS * u + QT * (h + 1))
                rows = slice(DH * h, DH * h + DH)
                for parts, stack, cols in ((q_parts, q_stack[n], slice(0, S)),
                                           (k_parts, k_stack[n], slice(HALO, HALO + S)),
                                           (d_parts, d_stack, slice(0, S // 2))):
                    at = 0
                    for part, count in ((0, 3), (1, 2), (2, 1)):
                        if parts is q_parts:
                            src = parts[rows, part:part + 1, :].to_broadcast([DH, count, S])
                        else:
                            src = parts[rows, 0:count, :]
                        sp.dma_start(stack[at:at + DH * count, h, cols], src).then_inc(s_stack[h], 16)
                        at += DH * count

            def store(b):
                wait_alone(sp, s_norm, QT * (b + 1))
                sp.dma_start(x_tiles(x1, b), y[:]).then_inc(s_store, 16)

            batches(sp, unit)
            store(B - 1)
            wait_alone(sp, s_store, 16 * B)

        @block.gpsimd
        def _(pool):
            n = 0

            def const(ins):
                nonlocal n
                n += 1
                ins.then_inc(s_const, 1)

            const(nc.gpsimd.memset(ident[:], 0.0))
            const(nc.gpsimd.memset(window[:], 1.0))
            pool.wait_ge(s_const, 2)
            const(nc.gpsimd.affine_select(out=ident[:], in_=ident[:], compare_op=ALU.not_equal, fill=1.0,
                                          base=0, pattern=[[-1, P]], channel_multiplier=1))
            const(nc.gpsimd.affine_select(out=window[:], in_=window[:], compare_op=ALU.is_ge, fill=0.0,
                                          base=0, pattern=[[-1, WIN]], channel_multiplier=1))
            pool.wait_ge(s_const, 4)
            const(nc.gpsimd.affine_select(out=window[:], in_=window[:], compare_op=ALU.is_ge, fill=0.0,
                                          base=WIN - 1, pattern=[[1, WIN]], channel_multiplier=-1))
            const(nc.gpsimd.memset(ones[:], 1.0))
            const(nc.gpsimd.memset(neg_half[:], -0.5))
            for g in (0, 1):
                const(nc.gpsimd.memset(k_stack[g][0:ROWS, :, 0:HALO], 0.0))
                const(nc.gpsimd.memset(k_stack[g][0:ROWS, :, HALO + S:KPAD], 0.0))
            pool.wait_ge(s_const, 11)
            for g in (0, 1):
                const(nc.gpsimd.memset(k_stack[g][SPLIT_ROWS:ROWS, :, HALO:HALO + S], 1.0))
            pool.wait_ge(s_const, 13)
            const(nc.gpsimd.memset(v_tiles[:, :, :, DH:DV], 1.0))
            pool.wait_ge(s_const, 14)
            const(nc.gpsimd.memset(v_tiles[0:HALO, 0, :, DH:DV], 0.0))
            pool.wait_ge(s_const, 15)
            const(nc.gpsimd.memset(v_tiles[HALO:64, VT - 1, :, DH:DV], 0.0))
            assert n == 16
            pool.wait_ge(s_const, 16)
            nc.gpsimd.memset(v_tiles[64:P, VT - 1, :, DH:DV], 0.0).then_inc(s_const, 1)

            def unit(b, g):
                cur, prev = flags(b, g)
                u = 2 * b + g
                if g == 1 and has(b, 0, B):
                    pool.wait_ge(s_jdone, before(ALL_JOBS, b, 1, 0))
                    wait(pool, s_tot, 8 * b)
                    alone(pool)
                    nc.gpsimd.tensor_copy(v_sum[1][:], v_sum[0][:]).then_inc(s_vsum1, 1)
                if g == 0 and has(b, 2, B + 1):
                    spread(b - 2)
                for s in range(STEPS):
                    for j, kind, i in jobs(b, g, s, 1):
                        if kind == "m":
                            pool.wait_ge(s_jdone, before(ALL_JOBS, b, g, j) + 1)
                            wait(pool, s_mrow, 48 * (u - 1))
                            alone(pool)
                            nc.gpsimd.tensor_copy(m_parts[:, 1, :], m_rest[:]).then_inc(s_mmid, 1)
                            pool.wait_ge(s_mmid, u)
                            nc.gpsimd.tensor_tensor(m_parts[:, 2, :], m_rest[:], m_parts[:, 1, :],
                                                    ALU.subtract).then_inc(s_mparts, 1)
                        if kind in PROJ:
                            k = before(PROJ, b, g, j)
                            parts = {"q": q_parts, "k": k_parts, "d": d_parts}[kind]
                            cols = slice(512 * i, 512 * i + 512)
                            pool.wait_ge(s_jdone, before(ALL_JOBS, b, g, j) + 1)
                            alone(pool)
                            nc.gpsimd.tensor_copy(parts[:, 1, cols], rest[:]).then_inc(s_mid, 1)
                            pool.wait_ge(s_mid, k + 1)
                            nc.gpsimd.tensor_tensor(parts[:, 2, cols], rest[:], parts[:, 1, cols],
                                                    ALU.subtract).then_inc(s_parts, 1)
                    if prev:
                        for h in late(s, 12):
                            if h % 2:
                                pair(b, g, h // 2)

            def pair(b, g, p):
                u = 2 * b + g
                o = 1 - g
                k = 4 * (u - 1) + p
                pool.wait_ge(s_inv, k + 1)
                if p == 0:
                    wait(pool, s_jdone, before(ALL_JOBS, b, g, JOBS[g].index("T1") + 1))
                t = total[:, p % 2].rearrange("p (a q) d -> p a q d", a=2)
                r = inv[:, p % 2].rearrange("p (a q) -> p a q", a=2).unsqueeze(3).to_broadcast([P, 2, QT, DH])
                dst = att[:, :, 32 * p:32 * p + 32].rearrange("p q (a d) -> p a q d", a=2)
                for a in (0, 1):
                    ins = nc.gpsimd.tensor_tensor(dst[:, a], t[:, a, :, 0:DH], r[:, a], ALU.mult)
                ins.then_inc(s_att, 1)

            def spread(b):
                pool.wait_ge(s_mv, QT * (b + 1))
                alone(pool)
                nc.gpsimd.tensor_scalar(var_eps[:], mean_var[:, :, 1], LN_EPS, None, ALU.add).then_inc(s_veps, 1)
                pool.wait_ge(s_veps, b + 1)
                nc.gpsimd.tensor_tensor(rstd[:], var_eps[:], neg_half[:], ALU.pow).then_inc(s_rstd, 1)

            batches(pool, unit)
            spread(B - 1)

        @block.tensor
        def _(pe):
            pe.wait_ge(s_const, 17)
            pe.wait_ge(s_wlo, 5)
            pe.wait_ge(s_whi, 5)

            def three(out, l_hi, l_lo, r_hi, r_lo, first, last):
                for n, (l, r) in enumerate(((l_hi, r_hi), (l_lo, r_hi), (l_hi, r_lo))):
                    ins = nc.tensor.matmul(out, l, r, start=first and n == 0, stop=last and n == 2)
                return ins

            def job(b, g, j, kind, i):
                u = 2 * b + g
                wait(pe, s_jdone, before(ALL_JOBS, b, g, j))
                if kind == "m":
                    pe.wait_ge(s_max, STEPS * u)
                    alone(pe)
                    ins = nc.tensor.transpose(p_job[0:64, 0:P], row_max[1 - g][:], ident[:])
                if kind == "T":
                    pe.wait_ge(s_att, 4 * (u - 1))
                    for q in range(4):
                        ins = nc.tensor.transpose(p_job[:, P * q:P * q + P], att[:, 4 * i + q, :], ident[:])
                if kind == "X":
                    pe.wait_ge(s_x, 16 * (b + 2))
                    c, half = i // 2, i % 2
                    for q in range(4):
                        ins = nc.tensor.transpose(p_job[:, P * q:P * q + P],
                                                  x_in[:, 4 * half + q, P * c:P * c + P], ident[:])
                if kind in PROJ:
                    n = 1 - g
                    for t, (w, half) in enumerate({"q": ((0, i),), "k": ((1, i),), "d": ((1, 0), (4, 1))}[kind]):
                        for c in (0, 1):
                            m = slice(P * n, P * n + P)
                            cols = slice(HALO + 512 * half, HALO + 512 * half + 512)
                            ins = three(p_job[:], w_hi[:, w, c, m], w_lo[:, w, c, m],
                                        xt_hi[:, c, cols], xt_lo[:, c, cols],
                                        t == 0 and c == 0, (kind != "d" or t == 1) and c == 1)
                if kind == "V":
                    for t in range(2 * i, min(2 * i + 2, VT)):
                        for c in (0, 1):
                            cols = slice(P * t, P * t + P)
                            ins = three(p_job[:, C * (t % 2):C * (t % 2) + C], xt_hi[:, c, cols],
                                        xt_lo[:, c, cols], w_hi[:, 2, c, :], w_lo[:, 2, c, :], c == 0, c == 1)
                if kind == "S":
                    for t in range(VT):
                        ins = nc.tensor.matmul(p_job[:, 0:C].rearrange("p (h d) -> p h d", d=DH), ones[:],
                                               v_tiles[:, t, :, 0:DH], start=t == 0, stop=t == VT - 1)
                if kind == "O":
                    for q in range(2 * i, 2 * i + 2):
                        for c in (0, 1):
                            cols = slice(P * q, P * q + P)
                            ins = three(p_job[:, C * (q % 2):C * (q % 2) + C], at_hi[:, c, cols],
                                        at_lo[:, c, cols], w_hi[:, 3, c, :], w_lo[:, 3, c, :], c == 0, c == 1)
                ins.then_inc(s_jmm, 1)

            def unit(b, g):
                cur, prev = flags(b, g)
                u = 2 * b + g
                for s in range(STEPS):
                    h, q = s // QT, s % QT
                    if cur:
                        k = STEPS * u + s
                        if q == 0:
                            pe.wait_ge(s_stack[h], STACK_INC * (u + 1))
                        wait(pe, s_above, k - 1)
                        qs = q_stack[g][0:SPLIT_ROWS, h, P * q:P * q + P]
                        nc.tensor.matmul(p_diff[s % 2][:], qs, d_stack[0:SPLIT_ROWS, h, :],
                                         start=True, stop=True).then_inc(s_diff, 1)
                        wait(pe, s_max, k - 1)
                        nc.tensor.matmul(p_half[s % 2][:], qs,
                                         k_stack[g][0:SPLIT_ROWS, h, HALO + S // 2:HALO + S],
                                         start=True, stop=True).then_inc(s_half, 1)
                    for j, kind, i in jobs(b, g, s, 0):
                        job(b, g, j, kind, i)
                    if prev:
                        for hh in late(s, 6):
                            window_scores(u, g, hh)
                        for hh in late(s, 11):
                            weighted_values(b, g, hh)

            def window_scores(u, g, h):
                o = 1 - g
                k = GH * (u - 1) + h
                if h == 0:
                    pe.wait_ge(s_mrow, 48 * u)
                wait(pe, s_ww, k)
                for i in range(NBLK):
                    cols = slice(WIN * i, WIN * i + WIN)
                    ins = nc.tensor.matmul(p_win[:, cols], k_stack[o][0:ROWS, h, WIN * i:WIN * i + P],
                                           q_stack[o][0:ROWS, h, cols], start=True, stop=True)
                ins.then_inc(s_win, 1)

            def weighted_values(b, g, h):
                u = 2 * b + g
                o = 1 - g
                k = GH * (u - 1) + h
                pe.wait_ge(s_ww, k + 1)
                if h == 0:
                    pe.wait_ge(s_vwin[o], 48 * (b + g))
                if h % 2 == 0:
                    wait(pe, s_tot, 4 * (u - 1) + h // 2)
                for i in range(NBLK):
                    at = 136 * (h % 2) + DV * (i // 2)
                    half = slice(64 * (i % 2), 64 * (i % 2) + 64)
                    ins = nc.tensor.matmul(p_pv[half, at:at + DV], w_win[:, h % 2, WIN * i:WIN * i + WIN],
                                           v_win[o][:, i, h, :], start=True, stop=True)
                ins.then_inc(s_pv, 1)

            batches(pe, unit)

        @block.scalar
        def _(act):
            act.wait_ge(s_w, 64)
            for i, (w, sign) in enumerate(((0, 1.0), (1, 1.0), (2, 1.0), (3, 1.0), (1, -1.0))):
                nc.scalar.activation(w_hi[:, i], w_raw[:, w], ACT.Copy, scale=sign).then_inc(s_whi, 1)

            def job(b, g, j, kind, i):
                u = 2 * b + g
                act.wait_ge(s_jmm, before(ALL_JOBS, b, g, j) + 1)
                if kind == "m":
                    wait(act, s_mrow, 48 * (u - 1))
                    nc.scalar.activation(m_parts[:, 0, :], p_job[0:64, 0:P], ACT.Copy,
                                         scale=-1.0).then_inc(s_jact, 1)
                if kind == "T":
                    nc.scalar.activation(at_hi[:, g, 512 * i:512 * i + 512], p_job[:], ACT.Copy).then_inc(s_jact, 1)
                if kind == "X":
                    at = HALO + 512 * (i % 2)
                    nc.scalar.activation(xt_hi[:, i // 2, at:at + 512], p_job[:], ACT.Copy).then_inc(s_jact, 1)
                if kind in PROJ:
                    if kind == "q" and i == 0:
                        for h in range(GH):
                            wait(act, s_stack[h], STACK_INC * (u + 1))
                    parts = {"q": q_parts, "k": k_parts, "d": d_parts}[kind]
                    nc.scalar.activation(parts[:, 0, 512 * i:512 * i + 512], p_job[:],
                                         ACT.Copy).then_inc(s_jact, 1)
                if kind == "V":
                    if i == 0:
                        for o in (0, 1):
                            wait(act, s_vwin[o], 48 * b)
                    n = min(2, VT - 2 * i)
                    nc.scalar.activation(
                        v_tiles[:, 2 * i:2 * i + n, :, 0:DH],
                        p_job[:, 0:C * n].rearrange("p (t h d) -> p t h d", d=DH, h=HEADS),
                        ACT.Copy).then_inc(s_jdone, 1)

            def unit(b, g):
                cur, prev = flags(b, g)
                u = 2 * b + g
                for s in range(STEPS):
                    if cur:
                        k = STEPS * u + s
                        act.wait_ge(s_diff, k + 1)
                        wait(act, s_max, k - 3)
                        nc.scalar.activation(above[:, s % 4], p_diff[s % 2][:], ACT.Relu).then_inc(s_above, 1)
                    for j, kind, i in jobs(b, g, s, 1):
                        if kind in SPLIT_JOBS + "V":
                            job(b, g, j, kind, i)
                    if prev:
                        for h in late(s, 7):
                            k = GH * (u - 1) + h
                            act.wait_ge(s_win, k + 1)
                            nc.scalar.activation(p_win[:], p_win[:], ACT.Exp, scale=DH ** -0.5).then_inc(s_e1, 1)
                            act.wait_ge(s_e1, k + 1)
                            nc.scalar.activation(p_win[:], p_win[:], ACT.Exp).then_inc(s_e2, 1)

            batches(act, unit)

        @block.vector
        def _(dve):
            nc.vector.memset(xt_hi[:, :, 0:HALO].bitcast(F32), 0.0)
            nc.vector.memset(xt_hi[:, :, HALO + S:XPAD].bitcast(F32), 0.0)
            nc.vector.memset(xt_lo[:, :, 0:HALO].bitcast(F32), 0.0)
            nc.vector.memset(xt_lo[:, :, HALO + S:XPAD].bitcast(F32), 0.0)
            nc.vector.memset(v_sum[0][:, :, DH:DV], float(S))
            for i, (w, op) in enumerate(((0, 0), (1, 0), (2, 0), (3, 0), (1, 1))):
                dve.wait_ge(s_whi, i + 1)
                if op == 0:
                    ins = nc.vector.tensor_tensor(w_lo[:, i], w_raw[:, w], w_hi[:, i].bitcast(F32), ALU.subtract)
                else:
                    ins = nc.vector.scalar_tensor_tensor(w_lo[:, i], w_raw[:, w], -1.0, w_hi[:, i].bitcast(F32),
                                                         ALU.mult, ALU.subtract)
                ins.then_inc(s_wlo, 1)

            def job(b, g, j, kind, i):
                u = 2 * b + g
                if kind in SPLIT_JOBS:
                    dve.wait_ge(s_jact, before(SPLIT_JOBS, b, g, j) + 1)
                else:
                    dve.wait_ge(s_jmm, before(ALL_JOBS, b, g, j) + 1)
                if kind == "m":
                    wait(dve, s_mparts, u - 1)
                    nc.vector.scalar_tensor_tensor(m_rest[:], p_job[0:64, 0:P], -1.0, m_parts[:, 0, :],
                                                   ALU.mult, ALU.subtract).then_inc(s_jdone, 1)
                if kind == "T":
                    nc.vector.tensor_tensor(at_lo[:, g, 512 * i:512 * i + 512], p_job[:],
                                            at_hi[:, g, 512 * i:512 * i + 512].bitcast(F32),
                                            ALU.subtract).then_inc(s_jdone, 1)
                if kind == "X":
                    at = HALO + 512 * (i % 2)
                    nc.vector.tensor_tensor(xt_lo[:, i // 2, at:at + 512], p_job[:],
                                            xt_hi[:, i // 2, at:at + 512].bitcast(F32),
                                            ALU.subtract).then_inc(s_jdone, 1)
                if kind in PROJ:
                    wait(dve, s_parts, before(PROJ, b, g, j))
                    parts = {"q": q_parts, "k": k_parts, "d": d_parts}[kind]
                    nc.vector.tensor_tensor(rest[:], p_job[:], parts[:, 0, 512 * i:512 * i + 512],
                                            ALU.subtract).then_inc(s_jdone, 1)
                if kind == "S":
                    wait(dve, s_vsum1, b)
                    nc.vector.tensor_copy(v_sum[0][:, :, 0:DH],
                                          p_job[:, 0:C].rearrange("p (h d) -> p h d", d=DH)).then_inc(s_jdone, 1)
                if kind == "O":
                    if i == 0:
                        dve.wait_ge(s_xres, 16 * b)
                    nc.vector.tensor_tensor(y[:, 2 * i:2 * i + 2].rearrange("p t c -> p (t c)"), p_job[:],
                                            y[:, 2 * i:2 * i + 2].rearrange("p t c -> p (t c)"),
                                            ALU.add).then_inc(s_jdone, 1)

                    for q in range(2 * i, 2 * i + 2):
                        dve.wait_ge(s_jdone, before(ALL_JOBS, b, g, j) + 1)
                        nc.vector.bn_stats(stats[:, q], y[:, q]).then_inc(s_stats, 1)
                    for q in range(2 * i, 2 * i + 2):
                        dve.wait_ge(s_stats, QT * (b - 1) + q + 1)
                        alone(dve)
                        nc.vector.bn_aggr(mean_var[:, q], stats[:, q]).then_inc(s_mv, 1)

            def normalise(b, q):
                dve.wait_ge(s_rstd, b + 1)
                nc.vector.tensor_scalar(y[:, q], y[:, q], mean_var[:, q, 0:1], rstd[:, q:q + 1],
                                        ALU.subtract, ALU.mult).then_inc(s_norm, 1)

            def unit(b, g):
                cur, prev = flags(b, g)
                u = 2 * b + g
                for s in range(STEPS):
                    h, q = s // QT, s % QT
                    if cur:
                        k = STEPS * u + s
                        dve.wait_ge(s_above, k + 1)
                        dve.wait_ge(s_half, k + 1)
                        alone(dve)
                        nc.vector.tensor_tensor_reduce(
                            out=above[:, s % 4], in0=p_half[s % 2][:], in1=above[:, s % 4], scale=1.0, scalar=-3.0e38,
                            op0=ALU.add, op1=ALU.max, accum_out=row_max[g][:, s:s + 1]).then_inc(s_max, 1)
                    if g == 0 and has(b, 2, B + 1) and 1 <= s <= QT:
                        normalise(b - 2, s - 1)
                    for j, kind, i in jobs(b, g, s, 1):
                        if kind != "V":
                            job(b, g, j, kind, i)
                    if prev:
                        for hh in late(s, 9):
                            k = GH * (u - 1) + hh
                            dve.wait_ge(s_e2, k + 1)
                            wait(dve, s_pv, k - 1)
                            nc.vector.scalar_tensor_tensor(
                                w_win[:, hh % 2].rearrange("p (i j) -> p i j", j=WIN),
                                p_win[:].rearrange("p (i j) -> p i j", j=WIN), 1.0,
                                window[:].unsqueeze(1).to_broadcast([P, NBLK, WIN]),
                                ALU.subtract, ALU.mult).then_inc(s_ww, 1)
                        for hh in late(s, 12):
                            if hh % 2:
                                pair(b, g, hh // 2)

            def pair(b, g, p):
                u = 2 * b + g
                o = 1 - g
                k = 4 * (u - 1) + p
                dve.wait_ge(s_pv, GH * (u - 1) + 2 * p + 2)
                wait(dve, s_att, k - 1)
                if p == 0 and o == 0:
                    dve.wait_ge(s_jdone, before(ALL_JOBS, b, 1, 0))
                if p == 0 and o == 1:
                    dve.wait_ge(s_vsum1, b)
                sums = v_sum[o][:, GH * o + 2 * p:GH * o + 2 * p + 2, :].unsqueeze(2).to_broadcast([P, 2, QT, DV])
                nc.vector.tensor_tensor(total[:, p % 2].rearrange("p (a q) d -> p a q d", a=2),
                                        p_pv[:, 0:2 * QT * DV].rearrange("p (a q d) -> p a q d", a=2, d=DV),
                                        sums, ALU.add).then_inc(s_tot, 1)
                dve.wait_ge(s_tot, k + 1)
                nc.vector.reciprocal(inv[:, p % 2], total[:, p % 2, :, DH]).then_inc(s_inv, 1)

            batches(dve, unit)
            for q in range(QT):
                normalise(B - 1, q)


NETS = 3
LEAVES, LEAF_W = 16, 64
HID = LEAVES * LEAF_W
MT = HID // P
NODES = LEAVES - 1
NODE_PAD = 16
SEL = 2 * LEAVES
FAR = 1.0e30
HALF = S // 2
ITEMS = [(n, t) for n in range(NETS) for t in (0, 1)]
R_JOBS = ["x0", "x1", "x2", "x3", "n0", "s0", "s1"]
R_AT = {2: 0, 3: 1, 4: 2, 5: 3, 6: 4, 8: 5, 9: 6}
A_STEPS = QT + 2
SET_STEPS = 7 + 2 * NETS
BIAS_STEPS = 2 + 13


def leaf_attention(nc, x1, nets, out):
    with ExitStack() as ctx:
        def sb(name, shape, dt=F32):
            return ctx.enter_context(nc.sbuf_tensor(name, shape, dt))

        def psum(name, shape):
            return ctx.enter_context(nc.psum_tensor(name, shape, F32))

        def sem(name):
            return ctx.enter_context(nc.semaphore(name))

        w1_hi = sb("w1_hi", [P, NETS, 2, HID], F32R)
        w1_lo = sb("w1_lo", [P, NETS, 2, HID], F32R)
        w2_hi = sb("w2_hi", [P, NETS, MT, C], F32R)
        w2_lo = sb("w2_lo", [P, NETS, MT, C], F32R)
        arena = nc.sbuf_base
        sb("arena", [P, 12288])

        def at(name, offset, shape, dt=F32):
            return nc.alloc_sbuf_tensor_at(name, shape, dt, offset=arena + offset)

        hid_hi = at("hid_hi", 0, [P, MT, HALF], F32R)
        hid_lo = at("hid_lo", 16384, [P, MT, HALF], F32R)
        pt_hi = at("pt_hi", 0, [P, 2, QT, P], F32R)
        pt_lo = at("pt_lo", 8192, [P, 2, QT, P], F32R)
        probs = at("probs", 16384, [P, 2, S])
        x_tile = at("x_tile", 24576, [P, 2, 2, C])
        go = at("go", 24576, [P, QT * NETS, NODE_PAD])
        level1 = at("level1", 26112, [P, QT * NETS, 2])
        level2 = at("level2", 26304, [P, QT * NETS, 4])
        sel = at("sel", 28672, [P, QT * NETS, SEL])
        level3 = at("level3", 31744, [P, QT * NETS, 8])
        val_hi = at("val_hi", 32768, [P, QT, C], F32R)
        val_lo = at("val_lo", 40960, [P, QT, C], F32R)
        stage = at("stage", 32768, [P, 2, S])
        node_raw = at("node_raw", 40960, [NETS * NODE_PAD, C])
        b2_raw = at("b2_raw", 41984, [NETS * SEL, C])
        b2_hi = at("b2_hi", 43008, [NETS * SEL, C], F32R)
        b2_lo = at("b2_lo", 44032, [NETS * SEL, C])
        b1_raw = at("b1_raw", 45056, [NETS * SEL, LEAF_W])
        b1_hi = at("b1_hi", 45312, [NETS * SEL, LEAF_W], F32R)
        b1_lo = at("b1_lo", 45568, [NETS * SEL, LEAF_W])
        b1_val = at("b1_val", 45824, [NETS * SEL, LEAF_W])
        is_hi = at("is_hi", 46080, [NETS * SEL, LEAVES])
        is_lo = at("is_lo", 46144, [NETS * SEL, LEAVES])
        is_any = at("is_any", 46208, [NETS * SEL, LEAVES])
        far = at("far", 46272, [NETS * SEL, LEAVES])
        row_hi = at("row_hi", 46336, [NETS * SEL, 1])
        row_lo = at("row_lo", 46368, [NETS * SEL, 1])
        xt_hi = sb("ln_xt_hi", [P, 2, S], F32R)
        xt_lo = sb("ln_xt_lo", [P, 2, S], F32R)
        qk_hi = sb("qk_hi", [P, 2, 2, S], F32R)
        qk_lo = sb("qk_lo", [P, 2, 2, S], F32R)
        ident = sb("ident2", [P, P])
        sel_t = sb("sel_t", [NETS * SEL, S], F32R)
        bias1 = sb("bias1", [NETS * SEL, LEAVES, LEAF_W], F32R)
        bias2 = sb("bias2", [NETS * SEL, C], F32R)
        node_hi = sb("node_hi", [P, 2, NETS * NODE_PAD], F32R)
        node_lo = sb("node_lo", [P, 2, NETS * NODE_PAD], F32R)
        node_b = sb("node_bias", [P, NETS, NODE_PAD])
        top = sb("top", [P, 2])
        neg_top = sb("neg_top", [P, 2])
        mass = sb("mass", [P, 2])
        inv_mass = sb("inv_mass", [P, 2])
        y = sb("sum2", [P, 4, C])
        stats = sb("stats2", [P, 2, 6])
        mean_var = sb("mean_var2", [P, 2, 2])
        var_eps = sb("var_eps2", [P, 2])
        rstd = sb("rstd2", [P, 2])
        neg_half = sb("neg_half2", [P, 1])
        p_pair = [psum(f"p_pair{i}", [P, S]) for i in (0, 1)]
        p_one = [psum(f"p_one{i}", [P, 512]) for i in (0, 1)]
        p_out = psum("p_out", [P, 512])
        p_route = psum("p_route", [P, 512])

        s_set = sem("setup_step")
        s_small = sem("biases_loaded")
        s_wl = [sem(f"weights_piece_loaded{i}") for i in (0, 1)]
        s_whi = sem("weights_piece_hi")
        s_wlo = sem("weights_piece_lo")
        s_bias = sem("bias_step")
        s_xl = [sem(f"x1_tiles_loaded{i}") for i in (0, 1)]
        s_rmm = sem("routing_products")
        s_ract = sem("routing_hi_part")
        s_rdone = sem("routing_bank_read")
        s_tree = sem("tree_step")
        s_h1 = sem("hidden_products")
        s_hhi = sem("hidden_hi")
        s_hlo = sem("hidden_lo")
        s_l2 = sem("second_layer_products")
        s_ohi = sem("second_layer_hi")
        s_olo = sem("second_layer_lo")
        s_sc = sem("scores")
        s_top = sem("score_max")
        s_ntop = sem("negated_max")
        s_ex = sem("exponentials")
        s_tr = sem("weights_transposed")
        s_phi = sem("weights_t_hi")
        s_plo = sem("weights_t_lo")
        s_av = sem("weighted_values")
        s_inv = sem("inverse_mass")
        s_res = [sem(f"residual_loaded{i}") for i in range(4)]
        s_y = sem("sum_ready")
        s_stats = sem("stats2_ready")
        s_mv = sem("mean_var2_ready")
        s_veps = sem("var_eps2_ready")
        s_rstd = sem("rstd2_ready")
        s_norm = sem("out_ready")
        s_store = [sem(f"out_stored{i}") for i in range(4)]

        block = ctx.enter_context(nc.Block())
        NR = len(R_JOBS)
        NI = len(ITEMS)
        TREE = 9

        def tiles(t, b, first, count):
            rows = t[bass.ds(b, 1), P * first:P * first + P * count, :]
            return rows.rearrange("o (t p) c -> p (o t) c", p=P)

        def batches(eng, batch):
            batch(0, True)
            with eng.Fori(1, B - 1) as b:
                batch(b, True)
            batch(B - 1, False)

        @block.sync
        def _(sp):
            def load_x(b, r):
                sp.dma_start(x_tile[:, r % 2], tiles(x1, b, 2 * r, 2)).then_inc(s_xl[r % 2], 16)

            sp.wait_ge(s_set, 3)
            for n, (node_w, nb, w1, b1, w2, b2) in enumerate(nets):
                sp.dma_start(node_raw[NODE_PAD * n:NODE_PAD * n + NODES, :], node_w).then_inc(s_small, 16)
                sp.dma_start(node_b[:, n, 0:NODES], nb.partition_broadcast(P)).then_inc(s_small, 16)
                for part in (0, 1):
                    rows = slice(SEL * n + LEAVES * part, SEL * n + LEAVES * part + LEAVES)
                    sp.dma_start(b1_raw[rows, :], b1).then_inc(s_small, 16)
                    sp.dma_start(b2_raw[rows, :], b2).then_inc(s_small, 16)
            load_x(0, 0)
            load_x(0, 1)

            def piece(k):
                n, part = k // 4, k % 4
                w1, w2 = nets[n][2], nets[n][4]
                wait(sp, s_wlo, k - 1)
                if part < 2:
                    src = w1[:, P * part:P * part + P, :].rearrange("l p h -> p l h")
                else:
                    rows = w2.rearrange("l h c -> (l h) c").rearrange("(m p) c -> p m c", p=P)
                    src = rows[:, 4 * (part - 2):4 * (part - 2) + 4, :]
                sp.dma_start(stage[:, k % 2].rearrange("p (a c) -> p a c", a=src.shape[1]), src)\
                  .then_inc(s_wl[k % 2], 16)

            piece(0)
            piece(1)
            for r in (2, 3):
                sp.wait_ge(s_rmm, 1 + r - 1)
                load_x(0, r)
            for k in range(2, 4 * NETS):
                piece(k)

            def batch(b, more):
                for k in range(QT):
                    wait_alone(sp, s_store[k % 4], 16 * (QT // 4 * b + k // 4))
                    sp.dma_start(y[:, k % 4:k % 4 + 1], tiles(x1, b, k, 1)).then_inc(s_res[k % 4], 16)
                    if k == 3:
                        wait_alone(sp, s_l2, NI * (b + 1))
                    if more and k == 3:
                        for r in range(4):
                            if r >= 2:
                                wait_alone(sp, s_rmm, 1 + NR * (b + 1) + r - 1)
                            load_x(b + 1, r)

            batches(sp, batch)

        @block.gpsimd
        def _(pool):
            nc.gpsimd.memset(ident[:], 0.0).then_inc(s_set, 1)
            nc.gpsimd.memset(node_raw[:], 0.0).then_inc(s_set, 1)
            nc.gpsimd.memset(node_b[:], 0.0).then_inc(s_set, 1)
            nc.gpsimd.memset(is_hi[:], 0.0).then_inc(s_set, 1)
            nc.gpsimd.memset(is_lo[:], 0.0).then_inc(s_set, 1)
            nc.gpsimd.memset(neg_half[:], -0.5).then_inc(s_set, 1)
            done = 6
            pool.wait_ge(s_set, done)
            nc.gpsimd.affine_select(out=ident[:], in_=ident[:], compare_op=ALU.not_equal, fill=1.0,
                                    base=0, pattern=[[-1, P]], channel_multiplier=1).then_inc(s_set, 1)
            for n in range(NETS):
                for part, t in ((0, is_hi), (1, is_lo)):
                    done += 1
                    pool.wait_ge(s_set, done)
                    nc.gpsimd.affine_select(out=t[:], in_=t[:], compare_op=ALU.not_equal, fill=1.0,
                                            base=-(SEL * n + LEAVES * part), pattern=[[-1, LEAVES]],
                                            channel_multiplier=1).then_inc(s_set, 1)

            def spread(b, k):
                pool.wait_ge(s_mv, QT * b + k + 1)
                alone(pool)
                nc.gpsimd.tensor_scalar(var_eps[:, k % 2:k % 2 + 1], mean_var[:, k % 2, 1:2], LN_EPS, None,
                                        ALU.add).then_inc(s_veps, 1)
                pool.wait_ge(s_veps, QT * b + k + 1)
                nc.gpsimd.tensor_tensor(rstd[:, k % 2:k % 2 + 1], var_eps[:, k % 2:k % 2 + 1], neg_half[:],
                                        ALU.pow).then_inc(s_rstd, 1)

            def store(b, k):
                wait_alone(pool, s_norm, QT * b + k + 1)
                pool.dma_start(tiles(out, b, k, 1), y[:, k % 4:k % 4 + 1]).then_inc(s_store[k % 4], 16)

            def batch(b, more):
                for k in range(QT):
                    spread(b, k)
                    if k >= 1:
                        store(b, k - 1)
                store(b, QT - 1)

            batches(pool, batch)
            for i in range(4):
                pool.wait_ge(s_store[i], 16 * B * QT // 4)

        @block.tensor
        def _(pe):
            def three(out_, l_hi, l_lo, r_hi, r_lo, first, last, skip=False):
                for n, (l, r) in enumerate(((l_hi, r_hi), (l_lo, r_hi), (l_hi, r_lo))):
                    ins = nc.tensor.matmul(out_, l, r, start=first and n == 0, stop=last and n == 2,
                                           skip_group_check=skip)
                return ins

            def route(b, r):
                kind, i = R_JOBS[r][0], int(R_JOBS[r][1])
                pe.wait_ge(s_rdone, 1 + NR * b + r)
                alone(pe)
                if kind == "x":
                    pe.wait_ge(s_xl[i % 2], 16 * (2 * b + i // 2 + 1))
                    alone(pe)
                    for c in (0, 1):
                        for t in (0, 1):
                            at = 2 * P * c + P * t
                            ins = nc.tensor.transpose(p_route[:, at:at + P], x_tile[:, i % 2, t, P * c:P * c + P],
                                                      ident[:])
                if kind == "n":
                    for t in range(QT):
                        cols = slice(P * t, P * t + P)
                        for c in (0, 1):
                            ins = three(p_route[:, 48 * t:48 * t + 48], xt_hi[:, c, cols], xt_lo[:, c, cols],
                                        node_hi[:, c, :], node_lo[:, c, :], c == 0, c == 1)
                if kind == "s":
                    pe.wait_ge(s_tree, TREE * (b + 1))
                    alone(pe)
                    for t in range(4):
                        src = sel[:, NETS * (4 * i + t):NETS * (4 * i + t) + NETS, :]
                        src = src.rearrange("p n l -> p (n l)")
                        ins = nc.tensor.transpose(p_route[0:NETS * SEL, P * t:P * t + P], src, ident[:])
                ins.then_inc(s_rmm, 1)

            def first_layer(b, i, m):
                n, t = ITEMS[i]
                if i == 0 and m < 2:
                    wait(pe, s_plo, 2 * QT * b)
                else:
                    pe.wait_ge(s_hlo, MT * (NI * b + i) + m - 1)
                rows = slice(SEL * n, SEL * n + SEL)
                cols = slice(HALF * t, HALF * t + HALF)
                units = slice(P * m, P * m + P)
                nc.tensor.matmul(p_one[m % 2][:], bias1[rows, 2 * m:2 * m + 2, :].rearrange("p l h -> p (l h)"),
                                 sel_t[rows, cols], start=True, stop=False)
                for c in (0, 1):
                    ins = three(p_one[m % 2][:], w1_hi[:, n, c, units], w1_lo[:, n, c, units],
                                xt_hi[:, c, cols], xt_lo[:, c, cols], False, c == 1)
                ins.then_inc(s_h1, 1)

            def second_layer(b, i, m):
                n, t = ITEMS[i]
                rows = slice(SEL * n, SEL * n + SEL)
                bank = p_pair[i % 2]
                if m == 0:
                    if i >= 2:
                        pe.wait_ge(s_olo, NI * b + i - 1)
                    else:
                        wait(pe, s_ex, QT * b)
                pe.wait_ge(s_hlo, MT * (NI * b + i) + m + 1)
                alone(pe)
                for d in range(2 if n < 2 else 4):
                    if n < 2:
                        o = bank[:, HALF * d:HALF * d + HALF]
                        chan = slice(P * d, P * d + P)
                        if m == 0:
                            nc.tensor.matmul(o, bias2[rows, chan], sel_t[rows, HALF * t:HALF * t + HALF],
                                             start=True, stop=False)
                        ins = three(o, w2_hi[:, n, m, chan], w2_lo[:, n, m, chan], hid_hi[:, m, :],
                                    hid_lo[:, m, :], False, m == MT - 1)
                    else:
                        o = bank[:, C * d:C * d + C]
                        tok = slice(P * d, P * d + P)
                        if m == 0:
                            nc.tensor.matmul(o, sel_t[rows, HALF * t + P * d:HALF * t + P * d + P], bias2[rows, :],
                                             start=d % 2 == 0, stop=False, skip_group_check=True)
                        ins = three(o, hid_hi[:, m, tok], hid_lo[:, m, tok], w2_hi[:, n, m, :], w2_lo[:, n, m, :],
                                    False, m == MT - 1, True)
                if m == MT - 1:
                    ins.then_inc(s_l2, 1)

            def scores(b, k):
                if k < 2:
                    pe.wait_ge(s_olo, NI * (b + 1))
                else:
                    pe.wait_ge(s_ex, QT * b + k - 1)
                for half in (0, 1):
                    for c in (0, 1):
                        q = slice(P * k, P * k + P)
                        keys = slice(HALF * half, HALF * half + HALF)
                        ins = three(p_pair[k % 2][:, keys], qk_hi[:, 0, c, q], qk_lo[:, 0, c, q],
                                    qk_hi[:, 1, c, keys], qk_lo[:, 1, c, keys], c == 0, c == 1)
                ins.then_inc(s_sc, 1)

            def transposes(b, k):
                pe.wait_ge(s_ex, QT * b + k + 1)
                alone(pe)
                for j in (0, 1):
                    if k == 0:
                        pe.wait_ge(s_hlo, MT * NI * (b + 1))
                    else:
                        pe.wait_ge(s_plo, 2 * (QT * b + k) + j - 1)
                    alone(pe)
                    for t in range(4):
                        at = HALF * j + P * t
                        ins = nc.tensor.transpose(p_one[j][:, P * t:P * t + P], probs[:, k % 2, at:at + P], ident[:])
                    ins.then_inc(s_tr, 1)

            def weighted_values(b, k):
                pe.wait_ge(s_plo, 2 * (QT * b + k + 1))
                wait(pe, s_y, QT * b + k)
                for t in range(QT):
                    ins = three(p_out[:, 0:C], pt_hi[:, k % 2, t, :], pt_lo[:, k % 2, t, :],
                                val_hi[:, t, :], val_lo[:, t, :], t == 0, t == QT - 1)
                ins.then_inc(s_av, 1)

            pe.wait_ge(s_small, 16 * 6 * NETS)
            pe.wait_ge(s_set, SET_STEPS)
            for c in (0, 1):
                ins = nc.tensor.transpose(p_route[:, 48 * c:48 * c + 48], node_raw[:, P * c:P * c + P],
                                          ident[0:48, 0:48])
            ins.then_inc(s_rmm, 1)
            for r in range(NR):
                route(0, r)
            pe.wait_ge(s_bias, BIAS_STEPS)

            def batch(b, more):
                pe.wait_ge(s_rdone, 1 + NR * (b + 1))
                alone(pe)
                start = isinstance(b, int) and b == 0
                if start:
                    pe.wait_ge(s_wlo, 2)
                for m in range(MT):
                    first_layer(b, 0, m)
                for i in range(NI):
                    if start:
                        pe.wait_ge(s_wlo, 4 * ITEMS[i][0] + 4)
                    if start and i + 1 < NI:
                        pe.wait_ge(s_wlo, 4 * ITEMS[i + 1][0] + 2)
                    for m in range(MT):
                        second_layer(b, i, m)
                        if i + 1 < NI:
                            first_layer(b, i + 1, m)
                for k in range(A_STEPS):
                    if k < QT:
                        scores(b, k)
                    if 1 <= k <= QT:
                        transposes(b, k - 1)
                    if more and k in R_AT:
                        route(b + 1, R_AT[k])
                    if k >= 2:
                        weighted_values(b, k - 2)

            batches(pe, batch)

        @block.scalar
        def _(act):
            act.wait_ge(s_small, 16 * 6 * NETS)
            nc.scalar.activation(b1_hi[:], b1_raw[:], ACT.Copy).then_inc(s_bias, 1)
            nc.scalar.activation(b2_hi[:], b2_raw[:], ACT.Copy).then_inc(s_bias, 1)
            act.wait_ge(s_rmm, 1)
            nc.scalar.activation(node_hi[:].rearrange("p c n -> p (c n)"), p_route[:, 0:96],
                                 ACT.Copy).then_inc(s_ract, 1)

            def route(b, r):
                kind, i = R_JOBS[r][0], int(R_JOBS[r][1])
                if kind == "n":
                    return
                act.wait_ge(s_rmm, 1 + NR * b + r + 1)
                if kind == "x":
                    nc.scalar.activation(xt_hi[:, :, 2 * P * i:2 * P * i + 2 * P],
                                         p_route[:].rearrange("p (c n) -> p c n", c=2), ACT.Copy).then_inc(s_ract, 1)
                else:
                    nc.scalar.activation(sel_t[:, 4 * P * i:4 * P * i + 4 * P], p_route[0:NETS * SEL, :],
                                         ACT.Copy).then_inc(s_rdone, 1)

            def piece(k):
                n, part = k // 4, k % 4
                act.wait_ge(s_wl[k % 2], 16 * (k // 2 + 1))
                if part < 2:
                    dst = w1_hi[:, n, part, :]
                else:
                    dst = w2_hi[:, n, 4 * (part - 2):4 * (part - 2) + 4, :].rearrange("p m c -> p (m c)")
                nc.scalar.activation(dst, stage[:, k % 2], ACT.Copy).then_inc(s_whi, 1)

            def hidden(b, i, m):
                act.wait_ge(s_h1, MT * (NI * b + i) + m + 1)
                nc.scalar.activation(hid_hi[:, m, :], p_one[m % 2][:], ACT.Relu).then_inc(s_hhi, 1)

            for r in range(3):
                route(0, r)
            piece(0)
            piece(1)
            for r in range(3, NR):
                route(0, r)
            piece(2)
            piece(3)

            def batch(b, more):
                start = isinstance(b, int) and b == 0
                for m in range(MT):
                    hidden(b, 0, m)
                for i in range(NI):
                    n, t = ITEMS[i]
                    for m in range(MT):
                        if start and t == 0 and n < 2 and m % 2 == 1:
                            piece(4 * (n + 1) + m // 2)
                        if m == MT - 1:
                            act.wait_ge(s_l2, NI * b + i + 1)
                            if n < 2:
                                nc.scalar.activation(qk_hi[:, n, :, HALF * t:HALF * t + HALF],
                                                     p_pair[i % 2][:].rearrange("p (d n) -> p d n", d=2),
                                                     ACT.Copy).then_inc(s_ohi, 1)
                            else:
                                nc.scalar.activation(val_hi[:, 4 * t:4 * t + 4, :].rearrange("p t c -> p (t c)"),
                                                     p_pair[i % 2][:], ACT.Copy).then_inc(s_ohi, 1)
                        if i + 1 < NI:
                            hidden(b, i + 1, m)
                for k in range(A_STEPS):
                    if 1 <= k <= QT:
                        for j in (0, 1):
                            act.wait_ge(s_tr, 2 * (QT * b + k - 1) + j + 1)
                            nc.scalar.activation(
                                pt_hi[:, (k - 1) % 2, 4 * j:4 * j + 4, :].rearrange("p k q -> p (k q)"),
                                p_one[j][:], ACT.Copy).then_inc(s_phi, 1)
                    if more and k in R_AT:
                        route(b + 1, R_AT[k])
                    if k < QT:
                        act.wait_ge(s_ntop, QT * b + k + 1)
                        wait(act, s_inv, QT * b + k - 1)
                        nc.scalar.activation(probs[:, k % 2], p_pair[k % 2][:], ACT.Exp,
                                             bias=neg_top[:, k % 2:k % 2 + 1], scale=C ** -0.5,
                                             accum_out=mass[:, k % 2:k % 2 + 1]).then_inc(s_ex, 1)

            batches(act, batch)

        @block.vector
        def _(dve):
            dve.wait_ge(s_bias, 2)
            dve.wait_ge(s_set, SET_STEPS)
            done = 2

            def step(ins):
                nonlocal done
                done += 1
                ins.then_inc(s_bias, 1)
                dve.wait_ge(s_bias, done)

            step(nc.vector.tensor_reduce(row_hi[:], is_hi[:], mybir.AxisListType.X, ALU.add))
            step(nc.vector.tensor_reduce(row_lo[:], is_lo[:], mybir.AxisListType.X, ALU.add))
            step(nc.vector.tensor_tensor(is_any[:], is_hi[:], is_lo[:], ALU.add))
            step(nc.vector.tensor_scalar(far[:], is_hi[:], row_hi[:], FAR, ALU.subtract, ALU.mult))
            step(nc.vector.tensor_tensor(b1_lo[:], b1_raw[:], b1_hi[:].bitcast(F32), ALU.subtract))
            step(nc.vector.tensor_scalar(b1_lo[:], b1_lo[:], row_lo[:], None, ALU.mult))
            step(nc.vector.scalar_tensor_tensor(b1_val[:], b1_hi[:].bitcast(F32), row_hi[:], b1_lo[:],
                                                ALU.mult, ALU.add))
            step(nc.vector.tensor_tensor(bias1[:],
                                         b1_val[:].unsqueeze(1).to_broadcast([NETS * SEL, LEAVES, LEAF_W]),
                                         is_any[:].unsqueeze(2).to_broadcast([NETS * SEL, LEAVES, LEAF_W]), ALU.mult))
            step(nc.vector.tensor_tensor(bias1[:], bias1[:].bitcast(F32),
                                         far[:].unsqueeze(2).to_broadcast([NETS * SEL, LEAVES, LEAF_W]), ALU.add))
            step(nc.vector.tensor_tensor(b2_lo[:], b2_raw[:], b2_hi[:].bitcast(F32), ALU.subtract))
            step(nc.vector.tensor_scalar(b2_lo[:], b2_lo[:], row_lo[:], None, ALU.mult))
            step(nc.vector.scalar_tensor_tensor(bias2[:], b2_hi[:].bitcast(F32), row_hi[:], b2_lo[:], ALU.mult, ALU.add))
            step(nc.vector.tensor_scalar(node_b[:], node_b[:], -1.0, None, ALU.mult))
            assert done == BIAS_STEPS
            dve.wait_ge(s_ract, 1)
            nc.vector.tensor_tensor(node_lo[:].rearrange("p c n -> p (c n)"), p_route[:, 0:96],
                                    node_hi[:].rearrange("p c n -> p (c n)").bitcast(F32),
                                    ALU.subtract).then_inc(s_rdone, 1)

            def route(b, r):
                kind, i = R_JOBS[r][0], int(R_JOBS[r][1])
                if kind == "x":
                    cols = slice(2 * P * i, 2 * P * i + 2 * P)
                    dve.wait_ge(s_ract, 1 + 4 * b + i + 1)
                    nc.vector.tensor_tensor(xt_lo[:, :, cols], p_route[:].rearrange("p (c n) -> p c n", c=2),
                                            xt_hi[:, :, cols].bitcast(F32), ALU.subtract).then_inc(s_rdone, 1)
                if kind == "n":
                    dve.wait_ge(s_rmm, 1 + NR * b + r + 1)
                    nc.vector.tensor_tensor(
                        go[:].rearrange("p (t n) k -> p t (n k)", n=NETS),
                        p_route[:, 0:48 * QT].rearrange("p (t k) -> p t k", t=QT),
                        node_b[:].rearrange("p n k -> p (n k)").unsqueeze(1).to_broadcast([P, QT, 48]),
                        ALU.is_ge).then_inc(s_rdone, 1)
                    dve.wait_ge(s_rdone, 1 + NR * b + r + 1)
                    tree(b)

            def tree(b):
                n = TREE * b

                def branch(parent, nodes, child):
                    nonlocal n
                    nc.vector.tensor_tensor(child[:, :, 1::2], parent, go[:, :, nodes], ALU.mult).then_inc(s_tree, 1)
                    n = n + 1
                    dve.wait_ge(s_tree, n)
                    nc.vector.tensor_tensor(child[:, :, 0::2], parent, child[:, :, 1::2],
                                            ALU.subtract).then_inc(s_tree, 1)
                    n = n + 1
                    dve.wait_ge(s_tree, n)

                nc.vector.tensor_copy(level1[:, :, 1:2], go[:, :, 0:1]).then_inc(s_tree, 1)
                nc.vector.tensor_scalar(level1[:, :, 0:1], go[:, :, 0:1], -1.0, 1.0,
                                        ALU.mult, ALU.add).then_inc(s_tree, 1)
                n = n + 2
                dve.wait_ge(s_tree, n)
                branch(level1[:], slice(1, 3), level2[:])
                branch(level2[:], slice(3, 7), level3[:])
                branch(level3[:], slice(7, 15), sel[:, :, 0:LEAVES])
                nc.vector.tensor_copy(sel[:, :, LEAVES:SEL], sel[:, :, 0:LEAVES]).then_inc(s_tree, 1)

            def piece(k):
                n, part = k // 4, k % 4
                dve.wait_ge(s_whi, k + 1)
                if part < 2:
                    hi, lo = w1_hi[:, n, part, :], w1_lo[:, n, part, :]
                else:
                    ms = slice(4 * (part - 2), 4 * (part - 2) + 4)
                    hi, lo = (w[:, n, ms, :].rearrange("p m c -> p (m c)") for w in (w2_hi, w2_lo))
                nc.vector.tensor_tensor(lo, stage[:, k % 2], hi.bitcast(F32), ALU.subtract).then_inc(s_wlo, 1)

            def hidden(b, i, m):
                dve.wait_ge(s_hhi, MT * (NI * b + i) + m + 1)
                nc.vector.scalar_tensor_tensor(hid_lo[:, m, :], p_one[m % 2][:], 0.0,
                                               hid_hi[:, m, :].bitcast(F32), ALU.max,
                                               ALU.subtract).then_inc(s_hlo, 1)

            for r in range(3):
                route(0, r)
            piece(0)
            piece(1)
            for r in range(3, NR):
                route(0, r)
            piece(2)
            piece(3)

            def normalise(b, k):
                dve.wait_ge(s_rstd, QT * b + k + 1)
                nc.vector.tensor_scalar(y[:, k % 4], y[:, k % 4], mean_var[:, k % 2, 0:1], rstd[:, k % 2:k % 2 + 1],
                                        ALU.subtract, ALU.mult).then_inc(s_norm, 1)

            def batch(b, more):
                start = isinstance(b, int) and b == 0
                for m in range(MT):
                    hidden(b, 0, m)
                for i in range(NI):
                    n, t = ITEMS[i]
                    for m in range(MT):
                        if start and t == 0 and n < 2 and m % 2 == 1:
                            piece(4 * (n + 1) + m // 2)
                        if m == MT - 1:
                            dve.wait_ge(s_ohi, NI * b + i + 1)
                            if n < 2:
                                cols = slice(HALF * t, HALF * t + HALF)
                                nc.vector.tensor_tensor(qk_lo[:, n, :, cols],
                                                        p_pair[i % 2][:].rearrange("p (d n) -> p d n", d=2),
                                                        qk_hi[:, n, :, cols].bitcast(F32),
                                                        ALU.subtract).then_inc(s_olo, 1)
                            else:
                                hi, lo = (v[:, 4 * t:4 * t + 4, :].rearrange("p t c -> p (t c)")
                                          for v in (val_hi, val_lo))
                                nc.vector.tensor_tensor(lo, p_pair[i % 2][:], hi.bitcast(F32),
                                                        ALU.subtract).then_inc(s_olo, 1)
                        if i + 1 < NI:
                            hidden(b, i + 1, m)
                for k in range(A_STEPS + 1):
                    if 1 <= k <= QT:
                        dve.wait_ge(s_ex, QT * b + k)
                        nc.vector.reciprocal(inv_mass[:, (k - 1) % 2:(k - 1) % 2 + 1],
                                             mass[:, (k - 1) % 2:(k - 1) % 2 + 1]).then_inc(s_inv, 1)
                    if k < QT:
                        dve.wait_ge(s_sc, QT * b + k + 1)
                        nc.vector.tensor_reduce(top[:, k % 2:k % 2 + 1], p_pair[k % 2][:],
                                                mybir.AxisListType.X, ALU.max).then_inc(s_top, 1)
                        dve.wait_ge(s_top, QT * b + k + 1)
                        nc.vector.tensor_scalar(neg_top[:, k % 2:k % 2 + 1], top[:, k % 2:k % 2 + 1],
                                                -(C ** -0.5), None, ALU.mult).then_inc(s_ntop, 1)
                    if 1 <= k <= QT:
                        for j in (0, 1):
                            hi, lo = (v[:, (k - 1) % 2, 4 * j:4 * j + 4, :].rearrange("p k q -> p (k q)")
                                      for v in (pt_hi, pt_lo))
                            dve.wait_ge(s_phi, 2 * (QT * b + k - 1) + j + 1)
                            nc.vector.tensor_tensor(lo, p_one[j][:], hi.bitcast(F32), ALU.subtract).then_inc(s_plo, 1)
                    if more and k in R_AT:
                        route(b + 1, R_AT[k])
                    if 2 <= k < A_STEPS:
                        q = k - 2
                        dve.wait_ge(s_av, QT * b + q + 1)
                        dve.wait_ge(s_res[q % 4], 16 * (QT // 4 * b + q // 4 + 1))
                        dve.wait_ge(s_inv, QT * b + q + 1)
                        nc.vector.scalar_tensor_tensor(y[:, q % 4], p_out[:, 0:C], inv_mass[:, q % 2:q % 2 + 1],
                                                       y[:, q % 4], ALU.mult, ALU.add).then_inc(s_y, 1)
                        dve.wait_ge(s_y, QT * b + q + 1)
                        nc.vector.bn_stats(stats[:, q % 2], y[:, q % 4]).then_inc(s_stats, 1)
                        dve.wait_ge(s_stats, QT * b + q + 1)
                        alone(dve)
                        nc.vector.bn_aggr(mean_var[:, q % 2], stats[:, q % 2]).then_inc(s_mv, 1)
                    if k >= 3:
                        normalise(b, k - 3)

            batches(dve, batch)


_IN1 = ["L0_attn_x", "L0_attn_Wq", "L0_attn_Wk", "L0_attn_Wv", "L0_attn_Wo"]
_IN2 = [f"L0_ffn_{n}_{w}" for n in "qkv" for w in ("node_w", "node_b", "w1", "b1", "w2", "b2")]


def kernel(**inputs):
    import numpy as np
    import concourse.bacc as bacc
    from concourse.bass_utils import run_bass_kernel_spmd

    nc = bacc.Bacc("TRN2", target_bir_lowering=False, num_devices=1)
    arrays, aps = {}, {}
    for name in _IN1 + _IN2:
        a = np.ascontiguousarray(inputs[name])
        arrays[f"in_{name}"] = a
        aps[name] = nc.dram_tensor(f"in_{name}", a.shape, mybir.dt.from_np(a.dtype), kind="ExternalInput").ap()
    x1 = nc.dram_tensor("x1", (B, S, C), F32).ap()
    out = nc.dram_tensor("out_0", (B, S, C), F32, kind="ExternalOutput").ap()
    window_attention(nc, *(aps[n] for n in _IN1), x1)
    leaf_attention(nc, x1, [[aps[n] for n in _IN2[6 * i:6 * i + 6]] for i in range(NETS)], out)
    return run_bass_kernel_spmd(nc, [arrays], core_ids=[0]).results[0]["out_0"]
```

```python
from contextlib import ExitStack

import concourse.bass as bass
from concourse import mybir
from concourse.alu_op_type import AluOpType as ALU

ACT = mybir.ActivationFunctionType
F32 = mybir.dt.float32
F32R = mybir.dt.float32r
BF16 = mybir.dt.bfloat16

P = 128
LN_EPS = 1e-5

B, S, C = 8, 1024, 256
HEADS, DH = 16, 16
WIN = 64
HALO = WIN // 2
QT = S // P
NBLK = S // WIN
GH = 8
DV = DH + 1
XPAD = HALO + S + (P - HALO)
VT = XPAD // P
KPAD = HALO + S + HALO
STEPS = GH * QT
SPLIT_ROWS = 6 * DH
ROWS = SPLIT_ROWS + 3

JOBS = {
    0: ["m", "V0", "V1", "T0", "T1", "q0", "q1", "k0", "k1", "d0", "V2", "V3", "V4", "S0", "X0", "X1"],
    1: ["m", "X2", "X3", "q0", "T0", "T1", "q1", "k0", "k1", "d0", "O0", "O1", "O2", "O3"],
}
PROJ = "qkd"
WIN_LAG, TOTAL_LAG, PAIR_LAG = 9, 18, 19
EXP_LAGS = 10, 11, 12, 13
WEIGHT_LAGS = 13, 14
PV_LAGS = 15, 16
STACK_INC = 16 * 6


def present(kind, b, g):
    u = 2 * b + g
    return {
        "m": 1 <= u <= 2 * B,
        "T": 2 <= u <= 2 * B + 1,
        "q": 0 <= u + 1 < 2 * B, "k": 0 <= u + 1 < 2 * B, "d": 0 <= u + 1 < 2 * B,
        "X": b + 1 < B,
        "V": 0 <= b < B, "S": 0 <= b < B,
        "O": 1 <= b <= B,
    }[kind]


def counted(kinds, b, g, j):
    n = 0
    for bb in range(-1, B + 1):
        for gg in (0, 1):
            for jj, name in enumerate(JOBS[gg]):
                if (bb, gg, jj) >= (b, g, j):
                    return n
                if name[0] in kinds and present(name[0], bb, gg):
                    n += 1
    return n


def before(kinds, b, g, j):
    if isinstance(b, int):
        return counted(kinds, b, g, j)
    return counted(kinds, 2, g, j) + (b - 2) * (counted(kinds, 3, 0, 0) - counted(kinds, 2, 0, 0))


ALL_JOBS = "mTqkXVSO"
SPLIT_JOBS = "mTqkX"


def wait(eng, sem, value):
    if isinstance(value, int) and value <= 0:
        return
    eng.wait_ge(sem, value)


def alone(eng):
    eng.nop(nofuse=True)


def wait_alone(eng, sem, value):
    if not isinstance(value, int) or value > 0:
        eng.wait_ge(sem, value)
        alone(eng)


def window_attention(nc, x, w_q, w_k, w_v, w_o, x1):
    with ExitStack() as ctx:
        def sb(name, shape, dt=F32):
            return ctx.enter_context(nc.sbuf_tensor(name, shape, dt))

        def psum(name, shape):
            return ctx.enter_context(nc.psum_tensor(name, shape, F32))

        def sem(name):
            return ctx.enter_context(nc.semaphore(name))

        ident = sb("ident", [P, P])
        ones = sb("ones", [P, 1])
        window = sb("window", [P, WIN])
        neg_half = sb("neg_half", [P, QT])
        w_hi = sb("w_hi", [P, 4, 2, C], F32R)
        w_lo = sb("w_lo", [P, 4, 2, C], F32R)
        x_in = sb("x_in", [P, QT, C])
        xt_hi = sb("xt_hi", [P, 2, XPAD], F32R)
        xt_lo = sb("xt_lo", [P, 2, XPAD], F32R)
        q_parts = sb("q_parts", [P, 4, S], BF16)
        k_parts = sb("k_parts", [P, 4, S], BF16)
        d_parts = sb("d_parts", [P, 4, S // 2], BF16)
        k_diff = d_parts[:, 2:4, :].rearrange("p a s -> p (a s)").bitcast(F32)
        rest = sb("rest", [P, S // 2])
        q_stack = [sb(f"q_stack{g}", [P, GH, S], BF16) for g in (0, 1)]
        k_stack = [sb(f"k_stack{g}", [P, GH, KPAD], BF16) for g in (0, 1)]
        d_stack = sb("d_stack", [P, GH, S // 2], BF16)
        above = sb("above", [P, 4, S // 2])
        row_max = [sb(f"row_max{g}", [P, STEPS]) for g in (0, 1)]
        m_parts = sb("m_parts", [STEPS, 3, P], BF16)
        m_rest = sb("m_rest", [STEPS, P])
        v_tiles = sb("v_tiles", [P, VT, HEADS, DV])
        v_win = [sb(f"v_win{g}", [P, NBLK, GH, DV]) for g in (0, 1)]
        v_sum = [sb("v_sum0", [P, HEADS, DV]), sb("v_sum1", [P, GH, DV])]
        w_win = sb("w_win", [P, 2, S])
        w_raw = w_win[:].rearrange("p n (a c) -> p n a c", c=C).rearrange("p n (m a) c -> p (n m) a c", a=2)
        total = sb("total", [P, 2, 2 * QT, DV])
        inv = sb("inv", [P, 2, 2 * QT])
        att = sb("att", [P, QT, P])
        at_hi = sb("at_hi", [P, 2, S], F32R)
        at_lo = sb("at_lo", [P, 2, S], F32R)
        y = x_in
        stats = sb("stats", [P, QT, 6])
        mean_var = sb("mean_var", [P, QT, 2])
        var_eps = sb("var_eps", [P, QT])
        rstd = sb("rstd", [P, QT])

        p_diff = [psum(f"p_diff{i}", [P, 512]) for i in (0, 1)]
        p_half = [psum(f"p_half{i}", [P, 512]) for i in (0, 1)]
        p_win = psum("p_win", [P, S])
        p_pv = psum("p_pv", [P, 512])
        p_job = psum("p_job", [P, 512])

        s_w = sem("weights_loaded")
        s_const = sem("constants_step")
        s_whi = sem("weights_hi")
        s_wlo = sem("weights_lo")
        s_x = sem("x_loaded")
        s_xres = sem("x_res_loaded")
        s_jmm = sem("job_products")
        s_jact = sem("job_hi_part")
        s_jdone = sem("job_results_out_of_the_bank")
        s_kfirst = sem("keys_first_half")
        s_kdiff = sem("keys_difference")
        s_dhi = sem("difference_hi")
        s_drest = sem("difference_rest")
        s_mid = sem("proj_mid")
        s_parts = sem("proj_parts")
        s_twice = sem("proj_part_copied")
        s_mmid = sem("max_mid")
        s_mparts = sem("max_parts")
        s_mrow = sem("max_rows_stored")
        s_stack = [sem(f"stack_loaded{h}") for h in range(GH)]
        s_diff = sem("diff_scores")
        s_half = sem("half_scores")
        s_above = sem("above_ready")
        s_max = sem("row_max_done")
        s_win = sem("window_scores")
        s_e1 = sem("first_exp")
        s_e2 = sem("second_exp")
        s_ww = sem("window_weights")
        s_pv = sem("pv_done")
        s_tot = sem("totals")
        s_inv = sem("inverse")
        s_att = sem("attention_pair")
        s_vsum1 = sem("v_sum_copied")
        s_vwin = [sem(f"v_win_loaded{g}") for g in (0, 1)]
        s_stats = sem("stats_ready")
        s_mv = sem("mean_var_ready")
        s_veps = sem("var_eps_ready")
        s_rstd = sem("rstd_ready")
        s_norm = sem("x1_ready")
        s_store = sem("x1_stored")

        block = ctx.enter_context(nc.Block())

        def x_tiles(t, b):
            return t[bass.ds(b, 1), :, :].rearrange("o (t p) c -> p (o t) c", p=P)

        def batches(eng, unit):
            unit(-1, 0)
            unit(-1, 1)
            unit(0, 0)
            unit(0, 1)
            unit(1, 0)
            unit(1, 1)
            with eng.Fori(2, B - 1) as b:
                unit(b, 0)
                unit(b, 1)
            unit(B - 1, 0)
            unit(B - 1, 1)
            unit(B, 0)
            unit(B, 1)

        def has(b, lo, hi):
            return (lo <= b < hi) if isinstance(b, int) else lo <= 2 and hi > 6

        def has_scores(b):
            return not isinstance(b, int) or 0 <= b < B

        def job_at(step, lag):
            s = step - 1 - lag
            return s // 4 if s >= 0 and s % 4 == 0 else None

        def jobs(b, g, step, lag):
            j = job_at(step, lag)
            if j is not None and j < len(JOBS[g]):
                name = JOBS[g][j]
                bb = b if isinstance(b, int) else 2
                if present(name[0], bb, g):
                    yield j, name[0], int(name[1:] or 0)

        def late(b, g, step, lag):
            u = 2 * b + g
            for age in (2, 1):
                if isinstance(b, int) and not 0 <= u - age < 2 * B:
                    continue
                drain = 3 if isinstance(b, int) and u - age == 2 * B - 1 and lag >= PV_LAGS[0] else 0
                for h in range(GH):
                    if QT * h + lag + drain == step + STEPS * (age - 1):
                        yield u - age, (g - age) % 2, h

        @block.sync
        def _(sp):
            for i, w in enumerate((w_q, w_k, w_v, w_o)):
                sp.dma_start(w_raw[:, i], w.rearrange("(a p) n -> p a n", p=P)).then_inc(s_w, 16)

            def unit(b, g):
                u = 2 * b + g
                if g == 1 and has(b, -1, 0):
                    wait_alone(sp, s_const, 17)
                if not isinstance(b, int) or 1 <= u <= 2 * B:
                    wait_alone(sp, s_mparts, u)
                    for part in range(3):
                        row = SPLIT_ROWS + part
                        sp.dma_start(q_stack[1 - g][row:row + 1, :, :],
                                     m_parts[:, part, :]).then_inc(s_mrow, 16)
                if g == 0 and has(b, -1, 0):
                    sp.dma_start(x_in[:], x_tiles(x, 0)).then_inc(s_x, 16)
                if g == 0 and has(b, 2, B + 1):
                    store(b - 2)
                    wait_alone(sp, s_store, 16 * (b - 1))
                if g == 0 and has(b, 0, B - 1):
                    wait_alone(sp, s_jmm, before(ALL_JOBS, b, 0, 0))
                    sp.dma_start(x_in[:], x_tiles(x, b + 1)).then_inc(s_x, 16)
                if g == 1 and has(b, 0, B):
                    values(b, 1)
                if g == 1 and isinstance(b, int) and b == B:
                    residual(b)
                for h in range(GH):
                    if g == 1 and h == 0 and has(b, 1, B):
                        residual(b)
                    if g == 0 and h == 6 and has(b, 0, B):
                        values(b, 0)
                    if not isinstance(b, int) or 0 <= u + 1 < 2 * B:
                        load_stack(b, g, h)

            def residual(b):
                wait_alone(sp, s_jmm, before(ALL_JOBS, b, 1, JOBS[1].index("X3") + 1))
                sp.dma_start(y[:], x_tiles(x, b - 1)).then_inc(s_xres, 16)

            def values(b, g):
                wait_alone(sp, s_jdone, before(ALL_JOBS, b, 0, JOBS[0].index("V4")) + 1)
                wait_alone(sp, s_pv, GH * (2 * b + g - 1))
                hs = slice(GH * g, GH * g + GH)
                sp.dma_start(v_win[g][:, 0::2], v_tiles[:, 0:VT - 1, hs]).then_inc(s_vwin[g], 16)
                sp.dma_start(v_win[g][0:64, 1::2], v_tiles[64:P, 0:VT - 1, hs]).then_inc(s_vwin[g], 16)
                sp.dma_start(v_win[g][64:P, 1::2], v_tiles[0:64, 1:VT, hs]).then_inc(s_vwin[g], 16)

            def load_stack(b, g, h):
                u = 2 * b + g
                n = 1 - g
                if h == 0:
                    wait_alone(sp, s_parts, 5 * (u + 2))
                    wait_alone(sp, s_twice, 5 * (u + 2))
                wait_alone(sp, s_win, GH * (u - 1) + h + 1)
                wait_alone(sp, s_diff, STEPS * u + QT * (h + 1))
                rows = slice(DH * h, DH * h + DH)
                half = SPLIT_ROWS // 2
                for parts, stack, cols in ((q_parts, q_stack[n], slice(0, S)),
                                           (k_parts, k_stack[n], slice(HALO, HALO + S)),
                                           (d_parts, d_stack, slice(0, S // 2))):
                    if parts is q_parts:
                        sources = parts[rows, 1:4, :], parts[rows, 0:3, :]
                    else:
                        sources = parts[rows, 0:1, :].to_broadcast([DH, 3, parts.shape[2]]), parts[rows, 1:4, :]
                    for i, src in enumerate(sources):
                        sp.dma_start(stack[half * i:half * i + half, h, cols], src).then_inc(s_stack[h], 16)

            def store(b):
                wait_alone(sp, s_norm, QT * (b + 1))
                sp.dma_start(x_tiles(x1, b), y[:]).then_inc(s_store, 16)

            batches(sp, unit)
            store(B - 1)
            wait_alone(sp, s_store, 16 * B)

        @block.gpsimd
        def _(pool):
            n = 0

            def const(ins):
                nonlocal n
                n += 1
                ins.then_inc(s_const, 1)

            const(nc.gpsimd.memset(ident[:], 0.0))
            const(nc.gpsimd.memset(window[:], 1.0))
            pool.wait_ge(s_const, 2)
            const(nc.gpsimd.affine_select(out=ident[:], in_=ident[:], compare_op=ALU.not_equal, fill=1.0,
                                          base=0, pattern=[[-1, P]], channel_multiplier=1))
            const(nc.gpsimd.affine_select(out=window[:], in_=window[:], compare_op=ALU.is_ge, fill=0.0,
                                          base=0, pattern=[[-1, WIN]], channel_multiplier=1))
            pool.wait_ge(s_const, 4)
            const(nc.gpsimd.affine_select(out=window[:], in_=window[:], compare_op=ALU.is_ge, fill=0.0,
                                          base=WIN - 1, pattern=[[1, WIN]], channel_multiplier=-1))
            const(nc.gpsimd.memset(ones[:], 1.0))
            const(nc.gpsimd.memset(neg_half[:], -0.5))
            for g in (0, 1):
                const(nc.gpsimd.memset(k_stack[g][0:ROWS, :, 0:HALO], 0.0))
                const(nc.gpsimd.memset(k_stack[g][0:ROWS, :, HALO + S:KPAD], 0.0))
            pool.wait_ge(s_const, 11)
            for g in (0, 1):
                const(nc.gpsimd.memset(k_stack[g][SPLIT_ROWS:ROWS, :, HALO:HALO + S], 1.0))
            pool.wait_ge(s_const, 13)
            const(nc.gpsimd.memset(v_tiles[:, :, :, DH:DV], 1.0))
            pool.wait_ge(s_const, 14)
            const(nc.gpsimd.memset(v_tiles[0:HALO, 0, :, DH:DV], 0.0))
            pool.wait_ge(s_const, 15)
            const(nc.gpsimd.memset(v_tiles[HALO:64, VT - 1, :, DH:DV], 0.0))
            assert n == 16
            pool.wait_ge(s_const, 16)
            nc.gpsimd.memset(v_tiles[64:P, VT - 1, :, DH:DV], 0.0).then_inc(s_const, 1)
            pool.wait_ge(s_const, 17)

            def unit(b, g):
                u = 2 * b + g
                if g == 0 and has(b, 2, B + 1):
                    spread(b - 2)
                for s in range(STEPS):
                    for j, kind, i in jobs(b, g, s, 3):
                        if kind == "m":
                            pool.wait_ge(s_jdone, before(ALL_JOBS, b, g, j) + 1)
                            wait(pool, s_mrow, 48 * (u - 1))
                            alone(pool)
                            nc.gpsimd.tensor_copy(m_parts[:, 1, :], m_rest[:]).then_inc(s_mmid, 1)
                            pool.wait_ge(s_mmid, u)
                            nc.gpsimd.tensor_tensor(m_parts[:, 2, :], m_rest[:], m_parts[:, 1, :],
                                                    ALU.subtract).then_inc(s_mparts, 1)
                        if kind in PROJ:
                            k = before(PROJ, b, g, j)
                            parts = {"q": q_parts, "k": k_parts, "d": d_parts}[kind]
                            low = 3 if kind == "q" else 1
                            cols = slice(512 * i, 512 * i + 512)
                            pool.wait_ge(s_mid, k + 1)
                            nc.gpsimd.tensor_tensor(parts[:, low, cols], rest[:], parts[:, 2, cols],
                                                    ALU.subtract).then_inc(s_parts, 1)
                    for w, o, h in late(b, g, s, PAIR_LAG):
                        if h % 2:
                            pair(b, g, w, h // 2)
                    if s == QT * (GH - 1) + PAIR_LAG - STEPS and g == 1 and has(b, 0, B):
                        pool.wait_ge(s_jdone, before(ALL_JOBS, b, 1, 0))
                        wait(pool, s_tot, 2 * GH * b)
                        alone(pool)
                        nc.gpsimd.tensor_copy(v_sum[1][:], v_sum[0][:, GH:HEADS, :]).then_inc(s_vsum1, 1)

            def pair(b, g, w, p):
                k = 4 * w + p
                pool.wait_ge(s_inv, k + 1)
                if p == 0:
                    wait(pool, s_jdone, before(ALL_JOBS, b, g, JOBS[g].index("T1") + 1))
                t = total[:, p % 2].rearrange("p (a q) d -> p a q d", a=2)
                r = inv[:, p % 2].rearrange("p (a q) -> p a q", a=2).unsqueeze(3).to_broadcast([P, 2, QT, DH])
                dst = att[:, :, 32 * p:32 * p + 32].rearrange("p q (a d) -> p a q d", a=2)
                for a in (0, 1):
                    ins = nc.gpsimd.tensor_tensor(dst[:, a], t[:, a, :, 0:DH], r[:, a], ALU.mult)
                ins.then_inc(s_att, 1)

            def spread(b):
                pool.wait_ge(s_mv, QT * (b + 1))
                alone(pool)
                nc.gpsimd.tensor_scalar(var_eps[:], mean_var[:, :, 1], LN_EPS, None, ALU.add).then_inc(s_veps, 1)
                pool.wait_ge(s_veps, b + 1)
                nc.gpsimd.tensor_tensor(rstd[:], var_eps[:], neg_half[:], ALU.pow).then_inc(s_rstd, 1)

            batches(pool, unit)
            spread(B - 1)

        @block.tensor
        def _(pe):
            pe.wait_ge(s_const, 3)

            def three(out, l_hi, l_lo, r_hi, r_lo, first, last):
                for n, (l, r) in enumerate(((l_hi, r_hi), (l_lo, r_hi), (l_hi, r_lo))):
                    ins = nc.tensor.matmul(out, l, r, start=first and n == 0, stop=last and n == 2)
                return ins

            def job(b, g, j, kind, i, part):
                u = 2 * b + g
                if part == 0:
                    wait(pe, s_jdone, before(ALL_JOBS, b, g, j))
                    if JOBS[g][j - 1] == "d0":
                        wait(pe, s_kdiff, before("d", b, g, j))
                    if kind == "m":
                        pe.wait_ge(s_max, STEPS * u)
                        alone(pe)
                    if kind == "T":
                        pe.wait_ge(s_att, 4 * (u - 1))
                    if kind == "X":
                        pe.wait_ge(s_x, 16 * (b + 2))
                if kind == "m" and part == 1:
                    ins = nc.tensor.transpose(p_job[0:64, 0:P], row_max[1 - g][:], ident[:])
                if kind == "T":
                    for q in (2 * part, 2 * part + 1):
                        ins = nc.tensor.transpose(p_job[:, P * q:P * q + P], att[:, 4 * i + q, :], ident[:])
                if kind == "X":
                    c, half = i // 2, i % 2
                    for q in (2 * part, 2 * part + 1):
                        ins = nc.tensor.transpose(p_job[:, P * q:P * q + P],
                                                  x_in[:, 4 * half + q, P * c:P * c + P], ident[:])
                if kind in "qk":
                    w, c = PROJ.index(kind), part
                    m = slice(P * (1 - g), P * (1 - g) + P)
                    cols = slice(HALO + 512 * i, HALO + 512 * i + 512)
                    ins = three(p_job[:], w_hi[:, w, c, m], w_lo[:, w, c, m],
                                xt_hi[:, c, cols], xt_lo[:, c, cols], c == 0, c == 1)
                if kind == "V" and (i < VT // 2 or part == 1):
                    t = 2 * i + (part if i < VT // 2 else 0)
                    for c in (0, 1):
                        cols = slice(P * t, P * t + P)
                        ins = three(p_job[:, C * (t % 2):C * (t % 2) + C], xt_hi[:, c, cols],
                                    xt_lo[:, c, cols], w_hi[:, 2, c, :], w_lo[:, 2, c, :], c == 0, c == 1)
                if kind == "S" and part == 1:
                    for t in range(VT):
                        ins = nc.tensor.matmul(p_job[:, 0:C].rearrange("p (h d) -> p h d", d=DH),
                                               ones[:].to_broadcast([P, P]),
                                               v_tiles[:, t, :, 0:DH], start=t == 0, stop=t == VT - 1)
                if kind == "O":
                    q = 2 * i + part
                    for c in (0, 1):
                        cols = slice(P * q, P * q + P)
                        ins = three(p_job[:, C * (q % 2):C * (q % 2) + C], at_hi[:, c, cols],
                                    at_lo[:, c, cols], w_hi[:, 3, c, :], w_lo[:, 3, c, :], c == 0, c == 1)
                if part == 1:
                    ins.then_inc(s_jmm, 1)

            def unit(b, g):
                cur = has_scores(b)
                u = 2 * b + g
                if g == 1 and has(b, -1, 0):
                    pe.wait_ge(s_wlo, 4)
                    pe.wait_ge(s_whi, 4)
                for s in range(STEPS):
                    if cur:
                        if s == 0:
                            scores(u, g, 0, s_diff)
                        if s + 1 < STEPS:
                            scores(u, g, s + 1, s_diff)
                        scores(u, g, s, s_half)
                    for part in (0, 1):
                        for j, kind, i in jobs(b, g, s, part):
                            if kind != "d":
                                job(b, g, j, kind, i, part)
                    for w, o, hh in late(b, g, s, WIN_LAG):
                        window_scores(w, o, hh)
                    for part in (0, 1):
                        for w, o, hh in late(b, g, s, PV_LAGS[part]):
                            weighted_values(w, o, hh, part)

            def scores(u, g, s, which):
                h, q = s // QT, s % QT
                k = STEPS * u + s
                qs = q_stack[g][0:SPLIT_ROWS, h, P * q:P * q + P]
                if which is s_diff:
                    if q == 0:
                        pe.wait_ge(s_stack[h], STACK_INC * (u + 1))
                    wait(pe, s_above, k - 1)
                    nc.tensor.matmul(p_diff[s % 2][:], qs, d_stack[0:SPLIT_ROWS, h, :],
                                     start=True, stop=True).then_inc(s_diff, 1)
                else:
                    wait(pe, s_max, k - 1)
                    nc.tensor.matmul(p_half[s % 2][:], qs,
                                     k_stack[g][0:SPLIT_ROWS, h, HALO + S // 2:HALO + S],
                                     start=True, stop=True).then_inc(s_half, 1)

            def window_scores(w, o, h):
                k = GH * w + h
                if h == 0:
                    pe.wait_ge(s_mrow, 48 * (w + 1))
                wait(pe, s_ww, 2 * k)
                for i in range(NBLK):
                    cols = slice(WIN * i, WIN * i + WIN)
                    ins = nc.tensor.matmul(p_win[:, cols], k_stack[o][0:ROWS, h, WIN * i:WIN * i + P],
                                           q_stack[o][0:ROWS, h, cols], start=True, stop=True)
                ins.then_inc(s_win, 1)

            def weighted_values(w, o, h, part):
                k = GH * w + h
                pe.wait_ge(s_ww, 2 * k + part + 1)
                if h == 0:
                    pe.wait_ge(s_vwin[o], 24 * (w - o) + 48)
                if part == 0:
                    wait(pe, s_tot, k)
                for t in range(QT // 2 * part, QT // 2 * part + QT // 2):
                    ins = nc.tensor.matmul(p_pv[:, 2 * DV * t:2 * DV * t + 2 * DV].rearrange("p (n d) -> p n d", n=2),
                                           w_win[:, h % 2, P * t:P * t + P],
                                           v_win[o][:, 2 * t:2 * t + 2, h, :], start=True, stop=True)
                if part == 1:
                    ins.then_inc(s_pv, 1)

            batches(pe, unit)

        @block.scalar
        def _(act):
            act.wait_ge(s_w, 64)
            for w in range(4):
                nc.scalar.activation(w_hi[:, w], w_raw[:, w], ACT.Copy).then_inc(s_whi, 1)

            def job(b, g, j, kind, i):
                u = 2 * b + g
                if kind == "d":
                    act.wait_ge(s_kdiff, before("d", b, g, j) + 1)
                    nc.scalar.activation(d_parts[:, 0, :], k_diff, ACT.Copy).then_inc(s_dhi, 1)
                    return
                act.wait_ge(s_jmm, before(ALL_JOBS, b, g, j) + 1)
                if kind == "m":
                    wait(act, s_mrow, 48 * (u - 1))
                    nc.scalar.activation(m_parts[:, 0, :], p_job[0:64, 0:P], ACT.Copy,
                                         scale=-1.0).then_inc(s_jact, 1)
                if kind == "T":
                    nc.scalar.activation(at_hi[:, g, 512 * i:512 * i + 512], p_job[:], ACT.Copy).then_inc(s_jact, 1)
                if kind == "X":
                    at = HALO + 512 * (i % 2)
                    nc.scalar.activation(xt_hi[:, i // 2, at:at + 512], p_job[:], ACT.Copy).then_inc(s_jact, 1)
                if kind in PROJ:
                    if kind == "q" and i == 0:
                        for h in range(GH):
                            wait(act, s_stack[h], STACK_INC * (u + 1))
                    parts = {"q": q_parts, "k": k_parts}[kind]
                    nc.scalar.activation(parts[:, int(kind == "q"), 512 * i:512 * i + 512], p_job[:],
                                         ACT.Copy).then_inc(s_jact, 1)
                    if kind == "k" and i == 0:
                        nc.scalar.activation(k_diff, p_job[:], ACT.Copy).then_inc(s_kfirst, 1)
                if kind == "V":
                    if i == 0:
                        for o in (0, 1):
                            wait(act, s_vwin[o], 48 * b)
                    n = min(2, VT - 2 * i)
                    nc.scalar.activation(
                        v_tiles[:, 2 * i:2 * i + n, :, 0:DH],
                        p_job[:, 0:C * n].rearrange("p (t h d) -> p t h d", d=DH, h=HEADS),
                        ACT.Copy).then_inc(s_jdone, 1)

            def unit(b, g):
                cur = has_scores(b)
                u = 2 * b + g
                for s in range(STEPS):
                    if cur:
                        k = STEPS * u + s
                        act.wait_ge(s_diff, k + 1)
                        wait(act, s_max, k - 3)
                        nc.scalar.activation(above[:, s % 4], p_diff[s % 2][:], ACT.Relu).then_inc(s_above, 1)
                    for j, kind, i in jobs(b, g, s, 2):
                        if kind in SPLIT_JOBS + "Vd":
                            job(b, g, j, kind, i)
                    for j, kind, i in jobs(b, g, s, 4):
                        if kind in PROJ:
                            if kind == "d":
                                act.wait_ge(s_drest, before("d", b, g, j) + 1)
                            else:
                                act.wait_ge(s_jdone, before(ALL_JOBS, b, g, j) + 1)
                            parts = {"q": q_parts, "k": k_parts, "d": d_parts}[kind]
                            nc.scalar.activation(parts[:, 2, 512 * i:512 * i + 512], rest[:],
                                                 ACT.Copy).then_inc(s_mid, 1)
                    for n in range(4):
                        for w, o, h in late(b, g, s, EXP_LAGS[n]):
                            exponential(GH * w + h, n // 2, n % 2)

            def exponential(k, again, bank):
                cols = slice(512 * bank, 512 * bank + 512)
                if again:
                    act.wait_ge(s_e1, 2 * k + bank + 1)
                    nc.scalar.activation(p_win[:, cols], p_win[:, cols], ACT.Exp).then_inc(s_e2, 1)
                else:
                    act.wait_ge(s_win, k + 1)
                    nc.scalar.activation(p_win[:, cols], p_win[:, cols], ACT.Exp, scale=DH ** -0.5).then_inc(s_e1, 1)

            batches(act, unit)

        @block.vector
        def _(dve):
            nc.vector.memset(xt_hi[:, :, 0:HALO].bitcast(F32), 0.0)
            nc.vector.memset(xt_hi[:, :, HALO + S:XPAD].bitcast(F32), 0.0)
            nc.vector.memset(xt_lo[:, :, 0:HALO].bitcast(F32), 0.0)
            nc.vector.memset(xt_lo[:, :, HALO + S:XPAD].bitcast(F32), 0.0)
            nc.vector.memset(v_sum[0][:, :, DH:DV], float(S))
            for w in range(4):
                dve.wait_ge(s_whi, w + 1)
                nc.vector.tensor_tensor(w_lo[:, w], w_raw[:, w], w_hi[:, w].bitcast(F32),
                                        ALU.subtract).then_inc(s_wlo, 1)

            def job(b, g, j, kind, i):
                u = 2 * b + g
                if kind == "d":
                    dve.wait_ge(s_dhi, before("d", b, g, j) + 1)
                    dve.wait_ge(s_parts, before(PROJ, b, g, j))
                    nc.vector.tensor_tensor(rest[:], k_diff, d_parts[:, 0, :], ALU.subtract).then_inc(s_drest, 1)
                elif kind in SPLIT_JOBS:
                    dve.wait_ge(s_jact, before(SPLIT_JOBS, b, g, j) + 1)
                else:
                    dve.wait_ge(s_jmm, before(ALL_JOBS, b, g, j) + 1)
                if kind == "m":
                    wait(dve, s_mparts, u - 1)
                    nc.vector.scalar_tensor_tensor(m_rest[:], p_job[0:64, 0:P], -1.0, m_parts[:, 0, :],
                                                   ALU.mult, ALU.subtract).then_inc(s_jdone, 1)
                if kind == "T":
                    nc.vector.tensor_tensor(at_lo[:, g, 512 * i:512 * i + 512], p_job[:],
                                            at_hi[:, g, 512 * i:512 * i + 512].bitcast(F32),
                                            ALU.subtract).then_inc(s_jdone, 1)
                if kind == "X":
                    at = HALO + 512 * (i % 2)
                    nc.vector.tensor_tensor(xt_lo[:, i // 2, at:at + 512], p_job[:],
                                            xt_hi[:, i // 2, at:at + 512].bitcast(F32),
                                            ALU.subtract).then_inc(s_jdone, 1)
                if kind in "qk":
                    if kind == "k" and i == 0:
                        dve.wait_ge(s_kfirst, before("d", b, g, j) + 1)
                    wait(dve, s_parts, before(PROJ, b, g, j))
                    parts = {"q": q_parts, "k": k_parts}[kind]
                    nc.vector.tensor_tensor(rest[:], p_job[:], parts[:, int(kind == "q"), 512 * i:512 * i + 512],
                                            ALU.subtract).then_inc(s_jdone, 1)
                    if kind == "k" and i == 1:
                        nc.vector.tensor_tensor(k_diff, k_diff, p_job[:], ALU.subtract).then_inc(s_kdiff, 1)
                if kind == "S":
                    wait(dve, s_vsum1, b)
                    nc.vector.tensor_copy(v_sum[0][:, :, 0:DH],
                                          p_job[:, 0:C].rearrange("p (h d) -> p h d", d=DH)).then_inc(s_jdone, 1)
                if kind == "O":
                    if i == 0:
                        dve.wait_ge(s_xres, 16 * b)
                    nc.vector.tensor_tensor(y[:, 2 * i:2 * i + 2].rearrange("p t c -> p (t c)"), p_job[:],
                                            y[:, 2 * i:2 * i + 2].rearrange("p t c -> p (t c)"),
                                            ALU.add).then_inc(s_jdone, 1)

                    for q in range(2 * i, 2 * i + 2):
                        dve.wait_ge(s_jdone, before(ALL_JOBS, b, g, j) + 1)
                        nc.vector.bn_stats(stats[:, q], y[:, q]).then_inc(s_stats, 1)
                    for q in range(2 * i, 2 * i + 2):
                        dve.wait_ge(s_stats, QT * (b - 1) + q + 1)
                        alone(dve)
                        nc.vector.bn_aggr(mean_var[:, q], stats[:, q]).then_inc(s_mv, 1)

            def normalise(b, q):
                dve.wait_ge(s_rstd, b + 1)
                nc.vector.tensor_scalar(y[:, q], y[:, q], mean_var[:, q, 0:1], rstd[:, q:q + 1],
                                        ALU.subtract, ALU.mult).then_inc(s_norm, 1)

            def unit(b, g):
                cur = has_scores(b)
                u = 2 * b + g
                for s in range(STEPS):
                    h, q = s // QT, s % QT
                    if cur:
                        k = STEPS * u + s
                        dve.wait_ge(s_above, k + 1)
                        dve.wait_ge(s_half, k + 1)
                        alone(dve)
                        nc.vector.tensor_tensor_reduce(
                            out=above[:, s % 4], in0=p_half[s % 2][:], in1=above[:, s % 4], scale=1.0, scalar=-3.0e38,
                            op0=ALU.add, op1=ALU.max, accum_out=row_max[g][:, s:s + 1]).then_inc(s_max, 1)
                    if g == 0 and has(b, 2, B + 1) and 1 <= s <= QT:
                        normalise(b - 2, s - 1)
                    for j, kind, i in jobs(b, g, s, 2):
                        if kind != "V":
                            job(b, g, j, kind, i)
                    for j, kind, i in jobs(b, g, s, 4):
                        if kind in PROJ:
                            dve.wait_ge(s_mid, before(PROJ, b, g, j) + 1)
                            parts = {"q": q_parts, "k": k_parts, "d": d_parts}[kind]
                            copy, of = (0, 1) if kind == "q" else (3, 2)
                            cols = slice(512 * i, 512 * i + 512)
                            nc.vector.tensor_copy(parts[:, copy, cols], parts[:, of, cols]).then_inc(s_twice, 1)
                    for n in (0, 1):
                        for w, o, hh in late(b, g, s, WEIGHT_LAGS[n]):
                            weights(GH * w + hh, hh, n)
                    for w, o, hh in late(b, g, s, TOTAL_LAG):
                        totals(b, w, o, hh)
                    for w, o, hh in late(b, g, s, PAIR_LAG):
                        if hh % 2:
                            k = GH * w + hh
                            dve.wait_ge(s_tot, k + 1)
                            nc.vector.reciprocal(inv[:, hh // 2 % 2],
                                                 total[:, hh // 2 % 2, :, DH]).then_inc(s_inv, 1)

            def weights(k, h, bank):
                cols = slice(512 * bank, 512 * bank + 512)
                dve.wait_ge(s_e2, 2 * k + bank + 1)
                wait(dve, s_pv, k - 1)
                nc.vector.scalar_tensor_tensor(
                    w_win[:, h % 2, cols].rearrange("p (i j) -> p i j", j=WIN),
                    p_win[:, cols].rearrange("p (i j) -> p i j", j=WIN), 1.0,
                    window[:].unsqueeze(1).to_broadcast([P, NBLK // 2, WIN]),
                    ALU.subtract, ALU.mult).then_inc(s_ww, 1)

            def totals(b, w, o, h):
                k = GH * w + h
                dve.wait_ge(s_pv, k + 1)
                if h % 2 == 0:
                    wait(dve, s_att, 4 * w + h // 2 - 1)
                if h == 0 and o == 0:
                    dve.wait_ge(s_jdone, before(ALL_JOBS, b, 1, 0))
                if h == 0 and o == 1:
                    dve.wait_ge(s_vsum1, b)
                bank = p_pv[:, 0:2 * QT * DV].rearrange("p (q n d) -> p q n d", n=2, d=DV)
                for n in (0, 1):
                    rows = slice(64 * n, 64 * n + 64)
                    ins = nc.vector.tensor_tensor(total[rows, h // 2 % 2, QT * (h % 2):QT * (h % 2) + QT, :],
                                                  bank[rows, :, n, :],
                                                  v_sum[o][rows, h, :].unsqueeze(1).to_broadcast([64, QT, DV]),
                                                  ALU.add)
                ins.then_inc(s_tot, 1)

            batches(dve, unit)
            for q in range(QT):
                normalise(B - 1, q)


NETS = 3
LEAVES, LEAF_W = 16, 64
HID = LEAVES * LEAF_W
MT = HID // P
NODES = LEAVES - 1
NODE_PAD = 16
SEL = 2 * LEAVES
FAR = 1.0e30
HALF = S // 2
ITEMS = [(n, t) for n in range(NETS) for t in (0, 1)]
R_JOBS = ["x0", "x1", "x2", "x3", "n0", "s0", "s1"]
R_AT = {2: 0, 3: 1, 4: 2, 5: 3, 6: 4, 8: 5, 9: 6}
A_STEPS = QT + 2
SET_STEPS = 7 + 2 * NETS
BIAS_STEPS = 2 + 13


def leaf_attention(nc, x1, nets, out):
    with ExitStack() as ctx:
        def sb(name, shape, dt=F32):
            return ctx.enter_context(nc.sbuf_tensor(name, shape, dt))

        def psum(name, shape):
            return ctx.enter_context(nc.psum_tensor(name, shape, F32))

        def sem(name):
            return ctx.enter_context(nc.semaphore(name))

        w1_hi = sb("w1_hi", [P, NETS, 2, HID], F32R)
        w1_lo = sb("w1_lo", [P, NETS, 2, HID], F32R)
        w2_hi = sb("w2_hi", [P, NETS, MT, C], F32R)
        w2_lo = sb("w2_lo", [P, NETS, MT, C], F32R)
        arena = nc.sbuf_base
        sb("arena", [P, 12288])

        def at(name, offset, shape, dt=F32):
            return nc.alloc_sbuf_tensor_at(name, shape, dt, offset=arena + offset)

        hid_hi = at("hid_hi", 0, [P, MT, HALF], F32R)
        hid_lo = at("hid_lo", 16384, [P, MT, HALF], F32R)
        pt_hi = at("pt_hi", 0, [P, 2, QT, P], F32R)
        pt_lo = at("pt_lo", 8192, [P, 2, QT, P], F32R)
        probs = at("probs", 16384, [P, 2, S])
        x_tile = at("x_tile", 24576, [P, 2, 2, C])
        go = at("go", 24576, [P, QT * NETS, NODE_PAD])
        level1 = at("level1", 26112, [P, QT * NETS, 2])
        level2 = at("level2", 26304, [P, QT * NETS, 4])
        sel = at("sel", 28672, [P, QT * NETS, SEL])
        level3 = at("level3", 31744, [P, QT * NETS, 8])
        val_hi = at("val_hi", 32768, [P, QT, C], F32R)
        val_lo = at("val_lo", 40960, [P, QT, C], F32R)
        stage = at("stage", 32768, [P, 2, S])
        node_raw = at("node_raw", 40960, [NETS * NODE_PAD, C])
        b2_raw = at("b2_raw", 41984, [NETS * SEL, C])
        b2_hi = at("b2_hi", 43008, [NETS * SEL, C], F32R)
        b2_lo = at("b2_lo", 44032, [NETS * SEL, C])
        b1_raw = at("b1_raw", 45056, [NETS * SEL, LEAF_W])
        b1_hi = at("b1_hi", 45312, [NETS * SEL, LEAF_W], F32R)
        b1_lo = at("b1_lo", 45568, [NETS * SEL, LEAF_W])
        b1_val = at("b1_val", 45824, [NETS * SEL, LEAF_W])
        is_hi = at("is_hi", 46080, [NETS * SEL, LEAVES])
        is_lo = at("is_lo", 46144, [NETS * SEL, LEAVES])
        is_any = at("is_any", 46208, [NETS * SEL, LEAVES])
        far = at("far", 46272, [NETS * SEL, LEAVES])
        row_hi = at("row_hi", 46336, [NETS * SEL, 1])
        row_lo = at("row_lo", 46368, [NETS * SEL, 1])
        xt_hi = sb("ln_xt_hi", [P, 2, S], F32R)
        xt_lo = sb("ln_xt_lo", [P, 2, S], F32R)
        qk_hi = sb("qk_hi", [P, 2, 2, S], F32R)
        qk_lo = sb("qk_lo", [P, 2, 2, S], F32R)
        ident = sb("ident2", [P, P])
        sel_t = sb("sel_t", [NETS * SEL, S], F32R)
        bias1 = sb("bias1", [NETS * SEL, LEAVES, LEAF_W], F32R)
        bias2 = sb("bias2", [NETS * SEL, C], F32R)
        node_hi = sb("node_hi", [P, 2, NETS * NODE_PAD], F32R)
        node_lo = sb("node_lo", [P, 2, NETS * NODE_PAD], F32R)
        node_b = sb("node_bias", [P, NETS, NODE_PAD])
        top = sb("top", [P, 2])
        neg_top = sb("neg_top", [P, 2])
        mass = sb("mass", [P, 2])
        inv_mass = sb("inv_mass", [P, 2])
        y = sb("sum2", [P, 4, C])
        stats = sb("stats2", [P, 2, 6])
        mean_var = sb("mean_var2", [P, 2, 2])
        var_eps = sb("var_eps2", [P, 2])
        rstd = sb("rstd2", [P, 2])
        neg_half = sb("neg_half2", [P, 1])
        p_pair = [psum(f"p_pair{i}", [P, S]) for i in (0, 1)]
        p_one = [psum(f"p_one{i}", [P, 512]) for i in (0, 1)]
        p_out = psum("p_out", [P, 512])
        p_route = psum("p_route", [P, 512])

        s_set = sem("setup_step")
        s_small = sem("biases_loaded")
        s_wl = [sem(f"weights_piece_loaded{i}") for i in (0, 1)]
        s_whi = sem("weights_piece_hi")
        s_wlo = sem("weights_piece_lo")
        s_bias = sem("bias_step")
        s_xl = [sem(f"x1_tiles_loaded{i}") for i in (0, 1)]
        s_rmm = sem("routing_products")
        s_ract = sem("routing_hi_part")
        s_rdone = sem("routing_bank_read")
        s_tree = sem("tree_step")
        s_h1 = sem("hidden_products")
        s_hhi = sem("hidden_hi")
        s_hlo = sem("hidden_lo")
        s_l2 = sem("second_layer_products")
        s_ohi = sem("second_layer_hi")
        s_olo = sem("second_layer_lo")
        s_sc = sem("scores")
        s_top = sem("score_max")
        s_ntop = sem("negated_max")
        s_ex = sem("exponentials")
        s_tr = sem("weights_transposed")
        s_phi = sem("weights_t_hi")
        s_plo = sem("weights_t_lo")
        s_av = sem("weighted_values")
        s_inv = sem("inverse_mass")
        s_res = [sem(f"residual_loaded{i}") for i in range(4)]
        s_y = sem("sum_ready")
        s_stats = sem("stats2_ready")
        s_mv = sem("mean_var2_ready")
        s_veps = sem("var_eps2_ready")
        s_rstd = sem("rstd2_ready")
        s_norm = sem("out_ready")
        s_store = [sem(f"out_stored{i}") for i in range(4)]

        block = ctx.enter_context(nc.Block())
        NR = len(R_JOBS)
        NI = len(ITEMS)
        TREE = 9

        def tiles(t, b, first, count):
            rows = t[bass.ds(b, 1), P * first:P * first + P * count, :]
            return rows.rearrange("o (t p) c -> p (o t) c", p=P)

        def batches(eng, batch):
            batch(0, True)
            with eng.Fori(1, B - 1) as b:
                batch(b, True)
            batch(B - 1, False)

        @block.sync
        def _(sp):
            def load_x(b, r):
                sp.dma_start(x_tile[:, r % 2], tiles(x1, b, 2 * r, 2)).then_inc(s_xl[r % 2], 16)

            sp.wait_ge(s_set, 3)
            for n, (node_w, nb, w1, b1, w2, b2) in enumerate(nets):
                sp.dma_start(node_raw[NODE_PAD * n:NODE_PAD * n + NODES, :], node_w).then_inc(s_small, 16)
                sp.dma_start(node_b[:, n, 0:NODES], nb.partition_broadcast(P)).then_inc(s_small, 16)
                for part in (0, 1):
                    rows = slice(SEL * n + LEAVES * part, SEL * n + LEAVES * part + LEAVES)
                    sp.dma_start(b1_raw[rows, :], b1).then_inc(s_small, 16)
                    sp.dma_start(b2_raw[rows, :], b2).then_inc(s_small, 16)
            load_x(0, 0)
            load_x(0, 1)

            def piece(k):
                n, part = k // 4, k % 4
                w1, w2 = nets[n][2], nets[n][4]
                wait(sp, s_wlo, k - 1)
                if part < 2:
                    src = w1[:, P * part:P * part + P, :].rearrange("l p h -> p l h")
                else:
                    rows = w2.rearrange("l h c -> (l h) c").rearrange("(m p) c -> p m c", p=P)
                    src = rows[:, 4 * (part - 2):4 * (part - 2) + 4, :]
                sp.dma_start(stage[:, k % 2].rearrange("p (a c) -> p a c", a=src.shape[1]), src)\
                  .then_inc(s_wl[k % 2], 16)

            piece(0)
            piece(1)
            for r in (2, 3):
                sp.wait_ge(s_rmm, 1 + r - 1)
                load_x(0, r)
            for k in range(2, 4 * NETS):
                piece(k)

            def batch(b, more):
                for k in range(QT):
                    wait_alone(sp, s_store[k % 4], 16 * (QT // 4 * b + k // 4))
                    sp.dma_start(y[:, k % 4:k % 4 + 1], tiles(x1, b, k, 1)).then_inc(s_res[k % 4], 16)
                    if k == 3:
                        wait_alone(sp, s_l2, NI * (b + 1))
                    if more and k == 3:
                        for r in range(4):
                            if r >= 2:
                                wait_alone(sp, s_rmm, 1 + NR * (b + 1) + r - 1)
                            load_x(b + 1, r)

            batches(sp, batch)

        @block.gpsimd
        def _(pool):
            nc.gpsimd.memset(ident[:], 0.0).then_inc(s_set, 1)
            nc.gpsimd.memset(node_raw[:], 0.0).then_inc(s_set, 1)
            nc.gpsimd.memset(node_b[:], 0.0).then_inc(s_set, 1)
            nc.gpsimd.memset(is_hi[:], 0.0).then_inc(s_set, 1)
            nc.gpsimd.memset(is_lo[:], 0.0).then_inc(s_set, 1)
            nc.gpsimd.memset(neg_half[:], -0.5).then_inc(s_set, 1)
            done = 6
            pool.wait_ge(s_set, done)
            nc.gpsimd.affine_select(out=ident[:], in_=ident[:], compare_op=ALU.not_equal, fill=1.0,
                                    base=0, pattern=[[-1, P]], channel_multiplier=1).then_inc(s_set, 1)
            for n in range(NETS):
                for part, t in ((0, is_hi), (1, is_lo)):
                    done += 1
                    pool.wait_ge(s_set, done)
                    nc.gpsimd.affine_select(out=t[:], in_=t[:], compare_op=ALU.not_equal, fill=1.0,
                                            base=-(SEL * n + LEAVES * part), pattern=[[-1, LEAVES]],
                                            channel_multiplier=1).then_inc(s_set, 1)

            def spread(b, k):
                pool.wait_ge(s_mv, QT * b + k + 1)
                alone(pool)
                nc.gpsimd.tensor_scalar(var_eps[:, k % 2:k % 2 + 1], mean_var[:, k % 2, 1:2], LN_EPS, None,
                                        ALU.add).then_inc(s_veps, 1)
                pool.wait_ge(s_veps, QT * b + k + 1)
                nc.gpsimd.tensor_tensor(rstd[:, k % 2:k % 2 + 1], var_eps[:, k % 2:k % 2 + 1], neg_half[:],
                                        ALU.pow).then_inc(s_rstd, 1)

            def store(b, k):
                wait_alone(pool, s_norm, QT * b + k + 1)
                pool.dma_start(tiles(out, b, k, 1), y[:, k % 4:k % 4 + 1]).then_inc(s_store[k % 4], 16)

            def batch(b, more):
                for k in range(QT):
                    spread(b, k)
                    if k >= 1:
                        store(b, k - 1)
                store(b, QT - 1)

            batches(pool, batch)
            for i in range(4):
                pool.wait_ge(s_store[i], 16 * B * QT // 4)

        @block.tensor
        def _(pe):
            def three(out_, l_hi, l_lo, r_hi, r_lo, first, last, skip=False):
                for n, (l, r) in enumerate(((l_hi, r_hi), (l_lo, r_hi), (l_hi, r_lo))):
                    ins = nc.tensor.matmul(out_, l, r, start=first and n == 0, stop=last and n == 2,
                                           skip_group_check=skip)
                return ins

            def route(b, r):
                kind, i = R_JOBS[r][0], int(R_JOBS[r][1])
                pe.wait_ge(s_rdone, 1 + NR * b + r)
                alone(pe)
                if kind == "x":
                    pe.wait_ge(s_xl[i % 2], 16 * (2 * b + i // 2 + 1))
                    alone(pe)
                    for c in (0, 1):
                        for t in (0, 1):
                            at = 2 * P * c + P * t
                            ins = nc.tensor.transpose(p_route[:, at:at + P], x_tile[:, i % 2, t, P * c:P * c + P],
                                                      ident[:])
                if kind == "n":
                    for t in range(QT):
                        cols = slice(P * t, P * t + P)
                        for c in (0, 1):
                            ins = three(p_route[:, 48 * t:48 * t + 48], xt_hi[:, c, cols], xt_lo[:, c, cols],
                                        node_hi[:, c, :], node_lo[:, c, :], c == 0, c == 1)
                if kind == "s":
                    pe.wait_ge(s_tree, TREE * (b + 1))
                    alone(pe)
                    for t in range(4):
                        src = sel[:, NETS * (4 * i + t):NETS * (4 * i + t) + NETS, :]
                        src = src.rearrange("p n l -> p (n l)")
                        ins = nc.tensor.transpose(p_route[0:NETS * SEL, P * t:P * t + P], src, ident[:])
                ins.then_inc(s_rmm, 1)

            def first_layer(b, i, m):
                n, t = ITEMS[i]
                if i == 0 and m < 2:
                    wait(pe, s_plo, 2 * QT * b)
                else:
                    pe.wait_ge(s_hlo, MT * (NI * b + i) + m - 1)
                rows = slice(SEL * n, SEL * n + SEL)
                cols = slice(HALF * t, HALF * t + HALF)
                units = slice(P * m, P * m + P)
                nc.tensor.matmul(p_one[m % 2][:], bias1[rows, 2 * m:2 * m + 2, :].rearrange("p l h -> p (l h)"),
                                 sel_t[rows, cols], start=True, stop=False)
                for c in (0, 1):
                    ins = three(p_one[m % 2][:], w1_hi[:, n, c, units], w1_lo[:, n, c, units],
                                xt_hi[:, c, cols], xt_lo[:, c, cols], False, c == 1)
                ins.then_inc(s_h1, 1)

            def second_layer(b, i, m):
                n, t = ITEMS[i]
                rows = slice(SEL * n, SEL * n + SEL)
                bank = p_pair[i % 2]
                if m == 0:
                    if i >= 2:
                        pe.wait_ge(s_olo, NI * b + i - 1)
                    else:
                        wait(pe, s_ex, QT * b)
                pe.wait_ge(s_hlo, MT * (NI * b + i) + m + 1)
                alone(pe)
                for d in range(2 if n < 2 else 4):
                    if n < 2:
                        o = bank[:, HALF * d:HALF * d + HALF]
                        chan = slice(P * d, P * d + P)
                        if m == 0:
                            nc.tensor.matmul(o, bias2[rows, chan], sel_t[rows, HALF * t:HALF * t + HALF],
                                             start=True, stop=False)
                        ins = three(o, w2_hi[:, n, m, chan], w2_lo[:, n, m, chan], hid_hi[:, m, :],
                                    hid_lo[:, m, :], False, m == MT - 1)
                    else:
                        o = bank[:, C * d:C * d + C]
                        tok = slice(P * d, P * d + P)
                        if m == 0:
                            nc.tensor.matmul(o, sel_t[rows, HALF * t + P * d:HALF * t + P * d + P], bias2[rows, :],
                                             start=d % 2 == 0, stop=False, skip_group_check=True)
                        ins = three(o, hid_hi[:, m, tok], hid_lo[:, m, tok], w2_hi[:, n, m, :], w2_lo[:, n, m, :],
                                    False, m == MT - 1, True)
                if m == MT - 1:
                    ins.then_inc(s_l2, 1)

            def scores(b, k):
                if k < 2:
                    pe.wait_ge(s_olo, NI * (b + 1))
                else:
                    pe.wait_ge(s_ex, QT * b + k - 1)
                for half in (0, 1):
                    for c in (0, 1):
                        q = slice(P * k, P * k + P)
                        keys = slice(HALF * half, HALF * half + HALF)
                        ins = three(p_pair[k % 2][:, keys], qk_hi[:, 0, c, q], qk_lo[:, 0, c, q],
                                    qk_hi[:, 1, c, keys], qk_lo[:, 1, c, keys], c == 0, c == 1)
                ins.then_inc(s_sc, 1)

            def transposes(b, k):
                pe.wait_ge(s_ex, QT * b + k + 1)
                alone(pe)
                for j in (0, 1):
                    if k == 0:
                        pe.wait_ge(s_hlo, MT * NI * (b + 1))
                    else:
                        pe.wait_ge(s_plo, 2 * (QT * b + k) + j - 1)
                    alone(pe)
                    for t in range(4):
                        at = HALF * j + P * t
                        ins = nc.tensor.transpose(p_one[j][:, P * t:P * t + P], probs[:, k % 2, at:at + P], ident[:])
                    ins.then_inc(s_tr, 1)

            def weighted_values(b, k):
                pe.wait_ge(s_plo, 2 * (QT * b + k + 1))
                wait(pe, s_y, QT * b + k)
                for t in range(QT):
                    ins = three(p_out[:, 0:C], pt_hi[:, k % 2, t, :], pt_lo[:, k % 2, t, :],
                                val_hi[:, t, :], val_lo[:, t, :], t == 0, t == QT - 1)
                ins.then_inc(s_av, 1)

            pe.wait_ge(s_small, 16 * 6 * NETS)
            pe.wait_ge(s_set, SET_STEPS)
            for c in (0, 1):
                ins = nc.tensor.transpose(p_route[:, 48 * c:48 * c + 48], node_raw[:, P * c:P * c + P],
                                          ident[0:48, 0:48])
            ins.then_inc(s_rmm, 1)
            for r in range(NR):
                route(0, r)
            pe.wait_ge(s_bias, BIAS_STEPS)

            def batch(b, more):
                pe.wait_ge(s_rdone, 1 + NR * (b + 1))
                alone(pe)
                start = isinstance(b, int) and b == 0
                if start:
                    pe.wait_ge(s_wlo, 2)
                for m in range(MT):
                    first_layer(b, 0, m)
                for i in range(NI):
                    if start:
                        pe.wait_ge(s_wlo, 4 * ITEMS[i][0] + 4)
                    if start and i + 1 < NI:
                        pe.wait_ge(s_wlo, 4 * ITEMS[i + 1][0] + 2)
                    for m in range(MT):
                        second_layer(b, i, m)
                        if i + 1 < NI:
                            first_layer(b, i + 1, m)
                for k in range(A_STEPS):
                    if k < QT:
                        scores(b, k)
                    if 1 <= k <= QT:
                        transposes(b, k - 1)
                    if more and k in R_AT:
                        route(b + 1, R_AT[k])
                    if k >= 2:
                        weighted_values(b, k - 2)

            batches(pe, batch)

        @block.scalar
        def _(act):
            act.wait_ge(s_small, 16 * 6 * NETS)
            nc.scalar.activation(b1_hi[:], b1_raw[:], ACT.Copy).then_inc(s_bias, 1)
            nc.scalar.activation(b2_hi[:], b2_raw[:], ACT.Copy).then_inc(s_bias, 1)
            act.wait_ge(s_rmm, 1)
            nc.scalar.activation(node_hi[:].rearrange("p c n -> p (c n)"), p_route[:, 0:96],
                                 ACT.Copy).then_inc(s_ract, 1)

            def route(b, r):
                kind, i = R_JOBS[r][0], int(R_JOBS[r][1])
                if kind == "n":
                    return
                act.wait_ge(s_rmm, 1 + NR * b + r + 1)
                if kind == "x":
                    nc.scalar.activation(xt_hi[:, :, 2 * P * i:2 * P * i + 2 * P],
                                         p_route[:].rearrange("p (c n) -> p c n", c=2), ACT.Copy).then_inc(s_ract, 1)
                else:
                    nc.scalar.activation(sel_t[:, 4 * P * i:4 * P * i + 4 * P], p_route[0:NETS * SEL, :],
                                         ACT.Copy).then_inc(s_rdone, 1)

            def piece(k):
                n, part = k // 4, k % 4
                act.wait_ge(s_wl[k % 2], 16 * (k // 2 + 1))
                if part < 2:
                    dst = w1_hi[:, n, part, :]
                else:
                    dst = w2_hi[:, n, 4 * (part - 2):4 * (part - 2) + 4, :].rearrange("p m c -> p (m c)")
                nc.scalar.activation(dst, stage[:, k % 2], ACT.Copy).then_inc(s_whi, 1)

            def hidden(b, i, m):
                act.wait_ge(s_h1, MT * (NI * b + i) + m + 1)
                nc.scalar.activation(hid_hi[:, m, :], p_one[m % 2][:], ACT.Relu).then_inc(s_hhi, 1)

            for r in range(3):
                route(0, r)
            piece(0)
            piece(1)
            for r in range(3, NR):
                route(0, r)
            piece(2)
            piece(3)

            def batch(b, more):
                start = isinstance(b, int) and b == 0
                for m in range(MT):
                    hidden(b, 0, m)
                for i in range(NI):
                    n, t = ITEMS[i]
                    for m in range(MT):
                        if start and t == 0 and n < 2 and m % 2 == 1:
                            piece(4 * (n + 1) + m // 2)
                        if m == MT - 1:
                            act.wait_ge(s_l2, NI * b + i + 1)
                            if n < 2:
                                nc.scalar.activation(qk_hi[:, n, :, HALF * t:HALF * t + HALF],
                                                     p_pair[i % 2][:].rearrange("p (d n) -> p d n", d=2),
                                                     ACT.Copy).then_inc(s_ohi, 1)
                            else:
                                nc.scalar.activation(val_hi[:, 4 * t:4 * t + 4, :].rearrange("p t c -> p (t c)"),
                                                     p_pair[i % 2][:], ACT.Copy).then_inc(s_ohi, 1)
                        if i + 1 < NI:
                            hidden(b, i + 1, m)
                for k in range(A_STEPS):
                    if 1 <= k <= QT:
                        for j in (0, 1):
                            act.wait_ge(s_tr, 2 * (QT * b + k - 1) + j + 1)
                            nc.scalar.activation(
                                pt_hi[:, (k - 1) % 2, 4 * j:4 * j + 4, :].rearrange("p k q -> p (k q)"),
                                p_one[j][:], ACT.Copy).then_inc(s_phi, 1)
                    if more and k in R_AT:
                        route(b + 1, R_AT[k])
                    if k < QT:
                        act.wait_ge(s_ntop, QT * b + k + 1)
                        wait(act, s_inv, QT * b + k - 1)
                        nc.scalar.activation(probs[:, k % 2], p_pair[k % 2][:], ACT.Exp,
                                             bias=neg_top[:, k % 2:k % 2 + 1], scale=C ** -0.5,
                                             accum_out=mass[:, k % 2:k % 2 + 1]).then_inc(s_ex, 1)

            batches(act, batch)

        @block.vector
        def _(dve):
            dve.wait_ge(s_bias, 2)
            dve.wait_ge(s_set, SET_STEPS)
            done = 2

            def step(ins):
                nonlocal done
                done += 1
                ins.then_inc(s_bias, 1)
                dve.wait_ge(s_bias, done)

            step(nc.vector.tensor_reduce(row_hi[:], is_hi[:], mybir.AxisListType.X, ALU.add))
            step(nc.vector.tensor_reduce(row_lo[:], is_lo[:], mybir.AxisListType.X, ALU.add))
            step(nc.vector.tensor_tensor(is_any[:], is_hi[:], is_lo[:], ALU.add))
            step(nc.vector.tensor_scalar(far[:], is_hi[:], row_hi[:], FAR, ALU.subtract, ALU.mult))
            step(nc.vector.tensor_tensor(b1_lo[:], b1_raw[:], b1_hi[:].bitcast(F32), ALU.subtract))
            step(nc.vector.tensor_scalar(b1_lo[:], b1_lo[:], row_lo[:], None, ALU.mult))
            step(nc.vector.scalar_tensor_tensor(b1_val[:], b1_hi[:].bitcast(F32), row_hi[:], b1_lo[:],
                                                ALU.mult, ALU.add))
            step(nc.vector.tensor_tensor(bias1[:],
                                         b1_val[:].unsqueeze(1).to_broadcast([NETS * SEL, LEAVES, LEAF_W]),
                                         is_any[:].unsqueeze(2).to_broadcast([NETS * SEL, LEAVES, LEAF_W]), ALU.mult))
            step(nc.vector.tensor_tensor(bias1[:], bias1[:].bitcast(F32),
                                         far[:].unsqueeze(2).to_broadcast([NETS * SEL, LEAVES, LEAF_W]), ALU.add))
            step(nc.vector.tensor_tensor(b2_lo[:], b2_raw[:], b2_hi[:].bitcast(F32), ALU.subtract))
            step(nc.vector.tensor_scalar(b2_lo[:], b2_lo[:], row_lo[:], None, ALU.mult))
            step(nc.vector.scalar_tensor_tensor(bias2[:], b2_hi[:].bitcast(F32), row_hi[:], b2_lo[:], ALU.mult, ALU.add))
            step(nc.vector.tensor_scalar(node_b[:], node_b[:], -1.0, None, ALU.mult))
            assert done == BIAS_STEPS
            dve.wait_ge(s_ract, 1)
            nc.vector.tensor_tensor(node_lo[:].rearrange("p c n -> p (c n)"), p_route[:, 0:96],
                                    node_hi[:].rearrange("p c n -> p (c n)").bitcast(F32),
                                    ALU.subtract).then_inc(s_rdone, 1)

            def route(b, r):
                kind, i = R_JOBS[r][0], int(R_JOBS[r][1])
                if kind == "x":
                    cols = slice(2 * P * i, 2 * P * i + 2 * P)
                    dve.wait_ge(s_ract, 1 + 4 * b + i + 1)
                    nc.vector.tensor_tensor(xt_lo[:, :, cols], p_route[:].rearrange("p (c n) -> p c n", c=2),
                                            xt_hi[:, :, cols].bitcast(F32), ALU.subtract).then_inc(s_rdone, 1)
                if kind == "n":
                    dve.wait_ge(s_rmm, 1 + NR * b + r + 1)
                    nc.vector.tensor_tensor(
                        go[:].rearrange("p (t n) k -> p t (n k)", n=NETS),
                        p_route[:, 0:48 * QT].rearrange("p (t k) -> p t k", t=QT),
                        node_b[:].rearrange("p n k -> p (n k)").unsqueeze(1).to_broadcast([P, QT, 48]),
                        ALU.is_ge).then_inc(s_rdone, 1)
                    dve.wait_ge(s_rdone, 1 + NR * b + r + 1)
                    tree(b)

            def tree(b):
                n = TREE * b

                def branch(parent, nodes, child):
                    nonlocal n
                    nc.vector.tensor_tensor(child[:, :, 1::2], parent, go[:, :, nodes], ALU.mult).then_inc(s_tree, 1)
                    n = n + 1
                    dve.wait_ge(s_tree, n)
                    nc.vector.tensor_tensor(child[:, :, 0::2], parent, child[:, :, 1::2],
                                            ALU.subtract).then_inc(s_tree, 1)
                    n = n + 1
                    dve.wait_ge(s_tree, n)

                nc.vector.tensor_copy(level1[:, :, 1:2], go[:, :, 0:1]).then_inc(s_tree, 1)
                nc.vector.tensor_scalar(level1[:, :, 0:1], go[:, :, 0:1], -1.0, 1.0,
                                        ALU.mult, ALU.add).then_inc(s_tree, 1)
                n = n + 2
                dve.wait_ge(s_tree, n)
                branch(level1[:], slice(1, 3), level2[:])
                branch(level2[:], slice(3, 7), level3[:])
                branch(level3[:], slice(7, 15), sel[:, :, 0:LEAVES])
                nc.vector.tensor_copy(sel[:, :, LEAVES:SEL], sel[:, :, 0:LEAVES]).then_inc(s_tree, 1)

            def piece(k):
                n, part = k // 4, k % 4
                dve.wait_ge(s_whi, k + 1)
                if part < 2:
                    hi, lo = w1_hi[:, n, part, :], w1_lo[:, n, part, :]
                else:
                    ms = slice(4 * (part - 2), 4 * (part - 2) + 4)
                    hi, lo = (w[:, n, ms, :].rearrange("p m c -> p (m c)") for w in (w2_hi, w2_lo))
                nc.vector.tensor_tensor(lo, stage[:, k % 2], hi.bitcast(F32), ALU.subtract).then_inc(s_wlo, 1)

            def hidden(b, i, m):
                dve.wait_ge(s_hhi, MT * (NI * b + i) + m + 1)
                nc.vector.scalar_tensor_tensor(hid_lo[:, m, :], p_one[m % 2][:], 0.0,
                                               hid_hi[:, m, :].bitcast(F32), ALU.max,
                                               ALU.subtract).then_inc(s_hlo, 1)

            for r in range(3):
                route(0, r)
            piece(0)
            piece(1)
            for r in range(3, NR):
                route(0, r)
            piece(2)
            piece(3)

            def normalise(b, k):
                dve.wait_ge(s_rstd, QT * b + k + 1)
                nc.vector.tensor_scalar(y[:, k % 4], y[:, k % 4], mean_var[:, k % 2, 0:1], rstd[:, k % 2:k % 2 + 1],
                                        ALU.subtract, ALU.mult).then_inc(s_norm, 1)

            def batch(b, more):
                start = isinstance(b, int) and b == 0
                for m in range(MT):
                    hidden(b, 0, m)
                for i in range(NI):
                    n, t = ITEMS[i]
                    for m in range(MT):
                        if start and t == 0 and n < 2 and m % 2 == 1:
                            piece(4 * (n + 1) + m // 2)
                        if m == MT - 1:
                            dve.wait_ge(s_ohi, NI * b + i + 1)
                            if n < 2:
                                cols = slice(HALF * t, HALF * t + HALF)
                                nc.vector.tensor_tensor(qk_lo[:, n, :, cols],
                                                        p_pair[i % 2][:].rearrange("p (d n) -> p d n", d=2),
                                                        qk_hi[:, n, :, cols].bitcast(F32),
                                                        ALU.subtract).then_inc(s_olo, 1)
                            else:
                                hi, lo = (v[:, 4 * t:4 * t + 4, :].rearrange("p t c -> p (t c)")
                                          for v in (val_hi, val_lo))
                                nc.vector.tensor_tensor(lo, p_pair[i % 2][:], hi.bitcast(F32),
                                                        ALU.subtract).then_inc(s_olo, 1)
                        if i + 1 < NI:
                            hidden(b, i + 1, m)
                for k in range(A_STEPS + 1):
                    if 1 <= k <= QT:
                        dve.wait_ge(s_ex, QT * b + k)
                        nc.vector.reciprocal(inv_mass[:, (k - 1) % 2:(k - 1) % 2 + 1],
                                             mass[:, (k - 1) % 2:(k - 1) % 2 + 1]).then_inc(s_inv, 1)
                    if k < QT:
                        dve.wait_ge(s_sc, QT * b + k + 1)
                        nc.vector.tensor_reduce(top[:, k % 2:k % 2 + 1], p_pair[k % 2][:],
                                                mybir.AxisListType.X, ALU.max).then_inc(s_top, 1)
                        dve.wait_ge(s_top, QT * b + k + 1)
                        nc.vector.tensor_scalar(neg_top[:, k % 2:k % 2 + 1], top[:, k % 2:k % 2 + 1],
                                                -(C ** -0.5), None, ALU.mult).then_inc(s_ntop, 1)
                    if 1 <= k <= QT:
                        for j in (0, 1):
                            hi, lo = (v[:, (k - 1) % 2, 4 * j:4 * j + 4, :].rearrange("p k q -> p (k q)")
                                      for v in (pt_hi, pt_lo))
                            dve.wait_ge(s_phi, 2 * (QT * b + k - 1) + j + 1)
                            nc.vector.tensor_tensor(lo, p_one[j][:], hi.bitcast(F32), ALU.subtract).then_inc(s_plo, 1)
                    if more and k in R_AT:
                        route(b + 1, R_AT[k])
                    if 2 <= k < A_STEPS:
                        q = k - 2
                        dve.wait_ge(s_av, QT * b + q + 1)
                        dve.wait_ge(s_res[q % 4], 16 * (QT // 4 * b + q // 4 + 1))
                        dve.wait_ge(s_inv, QT * b + q + 1)
                        nc.vector.scalar_tensor_tensor(y[:, q % 4], p_out[:, 0:C], inv_mass[:, q % 2:q % 2 + 1],
                                                       y[:, q % 4], ALU.mult, ALU.add).then_inc(s_y, 1)
                        dve.wait_ge(s_y, QT * b + q + 1)
                        nc.vector.bn_stats(stats[:, q % 2], y[:, q % 4]).then_inc(s_stats, 1)
                        dve.wait_ge(s_stats, QT * b + q + 1)
                        alone(dve)
                        nc.vector.bn_aggr(mean_var[:, q % 2], stats[:, q % 2]).then_inc(s_mv, 1)
                    if k >= 3:
                        normalise(b, k - 3)

            batches(dve, batch)


_IN1 = ["L0_attn_x", "L0_attn_Wq", "L0_attn_Wk", "L0_attn_Wv", "L0_attn_Wo"]
_IN2 = [f"L0_ffn_{n}_{w}" for n in "qkv" for w in ("node_w", "node_b", "w1", "b1", "w2", "b2")]


def kernel(**inputs):
    import numpy as np
    import concourse.bacc as bacc
    from concourse.bass_utils import run_bass_kernel_spmd

    nc = bacc.Bacc("TRN2", target_bir_lowering=False, num_devices=1)
    arrays, aps = {}, {}
    for name in _IN1 + _IN2:
        a = np.ascontiguousarray(inputs[name])
        arrays[f"in_{name}"] = a
        aps[name] = nc.dram_tensor(f"in_{name}", a.shape, mybir.dt.from_np(a.dtype), kind="ExternalInput").ap()
    x1 = nc.dram_tensor("x1", (B, S, C), F32).ap()
    out = nc.dram_tensor("out_0", (B, S, C), F32, kind="ExternalOutput").ap()
    window_attention(nc, *(aps[n] for n in _IN1), x1)
    leaf_attention(nc, x1, [[aps[n] for n in _IN2[6 * i:6 * i + 6]] for i in range(NETS)], out)
    return run_bass_kernel_spmd(nc, [arrays], core_ids=[0]).results[0]["out_0"]
```
